# Optimizing a Trainium2 kernel written in Bass

```python
import numpy as np
import jax
import jax.numpy as jnp

def _softmax(x, axis=-1):
    return jax.nn.softmax(x, axis=axis)
def _gelu(x):
    return jax.nn.gelu(x, approximate=True)
def _silu(x):
    return jax.nn.silu(x)
def _sigmoid(x):
    return jax.nn.sigmoid(x)
def _layernorm(x, axis=-1, eps=1e-5):
    m = jnp.mean(x, axis=axis, keepdims=True)
    v = jnp.var(x, axis=axis, keepdims=True)
    return (x - m) / jnp.sqrt(v + eps)
def _scatter_add(tgt, idx, src, axis=0):
    return tgt.at[idx].add(src)
def _segment_sum(src, seg, n):
    return jax.ops.segment_sum(src, seg, n)

kernel_name = 'mk_conv_seq_d2_conv_nchw256_95fe4f'

def setup_inputs(seed: int = 0):
    np.random.seed(seed)
    _w = jnp.asarray
    def _rec_inputs():
        import jax
        import jax.numpy as jnp
        _gk = jax.random.key(seed)
        x = -0.0002928 + 1 * jax.random.normal(jax.random.fold_in(_gk, 1), (4, 256, 64, 64), jnp.float32)
        return x
    x = _rec_inputs()
    def _L0_conv_setup():
        import jax, jax.numpy as jnp
        import numpy as np
        B, C, H, W = (4, 256, 64, 64)
        CQK = C // 8
        key = jax.random.key(seed)
        ks = jax.random.split(key, 4)
        scale = 0.02
        x = jax.random.normal(ks[0], (B, C, H, W), dtype=jnp.float32)
        Wq = jax.random.normal(ks[1], (CQK, C), dtype=jnp.float32) * scale
        bq = jnp.zeros((CQK,), dtype=jnp.float32)
        Wk = jax.random.normal(ks[2], (CQK, C), dtype=jnp.float32) * scale
        bk = jnp.zeros((CQK,), dtype=jnp.float32)
        Wv = jax.random.normal(ks[3], (C, C), dtype=jnp.float32) * scale
        bv = jnp.zeros((C,), dtype=jnp.float32)
        gamma = jnp.ones((1,), dtype=jnp.float32)
        return {'x': x, 'Wq': Wq, 'bq': bq, 'Wk': Wk, 'bk': bk, 'Wv': Wv, 'bv': bv, 'gamma': gamma}
    _L0_conv_all = _L0_conv_setup()
    _L0_conv_in = {k: v for k, v in _L0_conv_all.items() if k in ('Wq', 'bq', 'Wk', 'bk', 'Wv', 'bv', 'gamma', )}
    del _L0_conv_all

    def _L1_conv_setup():
        import jax, jax.numpy as jnp
        import numpy as np
        B, C, H, W = (8, 256, 64, 64)

        def conv1x1(x, w, b):
            return jnp.einsum('oc,nchw->nohw', w, x) + b[None, :, None, None]

        def maxpool2(x):
            return jax.lax.reduce_window(x, -jnp.inf, jax.lax.max, (1, 1, 2, 2), (1, 1, 2, 2), 'VALID')
        key = jax.random.key(seed)
        ks = jax.random.split(key, 10)
        d = C // 8
        dv = C // 2
        s = 0.05
        return {'x': jax.random.normal(ks[0], (B, C, H, W), jnp.float32), 'theta_w': jax.random.normal(ks[1], (d, C), jnp.float32) * s, 'theta_b': jax.random.normal(ks[2], (d,), jnp.float32) * s, 'phi_w': jax.random.normal(ks[3], (d, C), jnp.float32) * s, 'phi_b': jax.random.normal(ks[4], (d,), jnp.float32) * s, 'g_w': jax.random.normal(ks[5], (dv, C), jnp.float32) * s, 'g_b': jax.random.normal(ks[6], (dv,), jnp.float32) * s, 'out_w': jax.random.normal(ks[7], (C, dv), jnp.float32) * s, 'out_b': jax.random.normal(ks[8], (C,), jnp.float32) * s, 'gamma': jnp.array([0.3], jnp.float32)}
    _L1_conv_all = _L1_conv_setup()
    _L1_conv_in = {k: v for k, v in _L1_conv_all.items() if k in ('theta_w', 'theta_b', 'phi_w', 'phi_b', 'g_w', 'g_b', 'out_w', 'out_b', 'gamma', )}
    del _L1_conv_all

    return {
        "x": x,
        "L0_conv_Wq": _L0_conv_in["Wq"],
        "L0_conv_bq": _L0_conv_in["bq"],
        "L0_conv_Wk": _L0_conv_in["Wk"],
        "L0_conv_bk": _L0_conv_in["bk"],
        "L0_conv_Wv": _L0_conv_in["Wv"],
        "L0_conv_bv": _L0_conv_in["bv"],
        "L0_conv_gamma": _L0_conv_in["gamma"],
        "L1_conv_theta_w": _L1_conv_in["theta_w"],
        "L1_conv_theta_b": _L1_conv_in["theta_b"],
        "L1_conv_phi_w": _L1_conv_in["phi_w"],
        "L1_conv_phi_b": _L1_conv_in["phi_b"],
        "L1_conv_g_w": _L1_conv_in["g_w"],
        "L1_conv_g_b": _L1_conv_in["g_b"],
        "L1_conv_out_w": _L1_conv_in["out_w"],
        "L1_conv_out_b": _L1_conv_in["out_b"],
        "L1_conv_gamma": _L1_conv_in["gamma"],
    }

def reference(x, L0_conv_Wq, L0_conv_bq, L0_conv_Wk, L0_conv_bk, L0_conv_Wv, L0_conv_bv, L0_conv_gamma, L1_conv_theta_w, L1_conv_theta_b, L1_conv_phi_w, L1_conv_phi_b, L1_conv_g_w, L1_conv_g_b, L1_conv_out_w, L1_conv_out_b, L1_conv_gamma):
    import jax
    import jax.numpy as jnp
    def _L0_conv_ref(x, Wq, bq, Wk, bk, Wv, bv, gamma):
        import jax, jax.numpy as jnp
        import numpy as np
        B, C, H, W = (4, 256, 64, 64)
        CQK = C // 8
        b, c, h, w = x.shape
        n = h * w
        xf = x.reshape(b, c, n)
        q = jnp.einsum('oc,bcn->bon', Wq, xf) + bq[:, None]
        k = jnp.einsum('oc,bcn->bon', Wk, xf) + bk[:, None]
        v = jnp.einsum('oc,bcn->bon', Wv, xf) + bv[:, None]
        scores = jnp.einsum('bci,bcj->bij', q, k)
        attn = jax.nn.softmax(scores, axis=1)
        out = gamma * jnp.einsum('bcn,bnm->bcm', v, attn) + xf
        return out.reshape(b, c, h, w)

    def _L1_conv_ref(x, theta_w, theta_b, phi_w, phi_b, g_w, g_b, out_w, out_b, gamma):
        import jax, jax.numpy as jnp
        import numpy as np
        B, C, H, W = (8, 256, 64, 64)

        def conv1x1(x, w, b):
            return jnp.einsum('oc,nchw->nohw', w, x) + b[None, :, None, None]

        def maxpool2(x):
            return jax.lax.reduce_window(x, -jnp.inf, jax.lax.max, (1, 1, 2, 2), (1, 1, 2, 2), 'VALID')
        n, c, h, w = x.shape
        N, M = (h * w, h // 2 * (w // 2))
        theta = conv1x1(x, theta_w, theta_b).reshape(n, c // 8, N).transpose(0, 2, 1)
        phi = maxpool2(conv1x1(x, phi_w, phi_b)).reshape(n, c // 8, M)
        energy = jnp.einsum('nid,ndj->nij', theta, phi)
        attention = jax.nn.softmax(energy, axis=-1)
        g = maxpool2(conv1x1(x, g_w, g_b)).reshape(n, c // 2, M)
        out = jnp.einsum('ncj,nij->nci', g, attention)
        out = out.reshape(n, c // 2, h, w)
        out = conv1x1(out, out_w, out_b)
        return gamma * out + x

    def _gn(v, G=32, eps=1e-5):
        B_, C_, H_, W_ = v.shape
        g = v.reshape(B_, G, C_ // G, H_, W_)
        m = jnp.mean(g, axis=(2, 3, 4), keepdims=True)
        s = jnp.var(g, axis=(2, 3, 4), keepdims=True)
        return ((g - m) / jnp.sqrt(s + eps)).reshape(v.shape)

    def _ln_c(v, eps=1e-6):
        m = jnp.mean(v, axis=1, keepdims=True)
        s = jnp.var(v, axis=1, keepdims=True)
        return (v - m) / jnp.sqrt(s + eps)

    def _ln_t(v, eps=1e-5):
        m = jnp.mean(v, axis=-1, keepdims=True)
        s = jnp.var(v, axis=-1, keepdims=True)
        return (v - m) / jnp.sqrt(s + eps)

    def _to_tokens(v):
        B_, C_, H_, W_ = v.shape
        return v.reshape(B_, C_, H_ * W_).transpose(0, 2, 1)
    def _from_tokens(t, like):
        B_, C_, H_, W_ = like.shape
        return t.transpose(0, 2, 1).reshape(B_, C_, H_, W_)

    x = _L0_conv_ref(x, L0_conv_Wq, L0_conv_bq, L0_conv_Wk, L0_conv_bk, L0_conv_Wv, L0_conv_bv, L0_conv_gamma)
    x = _L1_conv_ref(x, L1_conv_theta_w, L1_conv_theta_b, L1_conv_phi_w, L1_conv_phi_b, L1_conv_g_w, L1_conv_g_b, L1_conv_out_w, L1_conv_out_b, L1_conv_gamma)
    return x


_drawn_inputs = setup_inputs


def setup_inputs(seed=0):
    import zlib

    import numpy as np

    out = dict(_drawn_inputs(seed))
    spreads = {'L0_conv_bq': (0.0, 0.8), 'L0_conv_bk': (0.0, 0.8), 'L0_conv_bv': (0.0, 0.1)}
    factors = {'L0_conv_Wq': 4.597,
     'L0_conv_Wk': 4.713,
     'L0_conv_Wv': 4.238,
     'L1_conv_theta_b': 8.0,
     'L1_conv_phi_b': 8.0,
     'L1_conv_g_b': 6.535,
     'L1_conv_out_b': 3.998}
    for name, (base, spread) in spreads.items():
        noise = np.random.default_rng([zlib.crc32(name.encode()), seed]).standard_normal(out[name].shape)
        drawn = base * np.exp(spread * noise) if base else spread * noise
        out[name] = jnp.asarray(drawn.astype(out[name].dtype))
    for name, factor in factors.items():
        out[name] = (out[name] * factor).astype(out[name].dtype)
    return out
```

```python
from contextlib import ExitStack

import concourse.bass as bass
from concourse import mybir

B, C, N = 4, 256, 4096
P = 128
DK = C // 8
DV = C // 2
CT = C // P
R3 = 3 * DK
CH = 512
NCH = N // CH
SUBS = CH // P
IMG_W = 64
PW = IMG_W // 2
CHROWS = CH // IMG_W
KEYS = (N, N // 4)
KT = tuple(k // P for k in KEYS)
STEPS = tuple(t // 2 for t in KT)
DIST = (1, 2)
VT = (CT, 1)
NST = tuple(SUBS * k // CH for k in KEYS)
NEP = (2, 4)
WCOLS = 4 * R3 + C + DV
W_Q, W_K, W_V, W_PHI, W_TH, W_G = 0, R3, 2 * R3, 2 * R3 + C, 3 * R3 + C, 4 * R3 + C
COL_BQ, COL_BK, COL_BPHI, COL_BTH, COL_BV, COL_BG, COL_BO, COL_G0, COL_G1 = 0, 1, 2, 3, 4, 6, 7, 9, 10
NCOLS = 11

STEP_BATCH = NCH * sum(STEPS)
CHUNK_BATCH = 2 * NCH
AUX_CHUNK = tuple(NST[i] + 1 + NEP[i] for i in range(2))
AUX_BATCH = NCH * sum(AUX_CHUNK)
HI_CHUNK = (4, 3)
HI_BATCH = NCH * sum(HI_CHUNK)
CREDIT = 8
AUX_CREDIT = 1
O_CREDIT = 1


def step_no(l, b, n, s):
    return b * STEP_BATCH + (l * NCH * STEPS[0] + s) + n * STEPS[l]


def chunk_no(l, b, n):
    return b * CHUNK_BATCH + n + l * NCH


def aux_base(l, b, n):
    off = l * NCH * AUX_CHUNK[0] + DIST[l] * (NST[l] + 1)
    if isinstance(n, int) and n == 0:
        return b * AUX_BATCH + off
    off += NST[l] + 1
    full = NCH - 1 - DIST[l]
    if isinstance(n, int) and n > full + 1:
        return b * AUX_BATCH + (off + full * AUX_CHUNK[l] + (n - 1 - full) * NEP[l])
    return b * AUX_BATCH + off + (n - 1) * AUX_CHUNK[l]


def hi_no(l, b, c, k):
    return b * HI_BATCH + (l * NCH * HI_CHUNK[0] + k) + c * HI_CHUNK[l]


def schedule(l, kind):
    ep = [] if kind == "first" else [("D1", 0), ("D2", 0), ("Z", 0), ("Z", 1)][:NEP[l]]
    st = [] if kind == "last" else [("ST", k) for k in range(NST[l])]
    per = ([2, 2] + [3, 2, 2] * 4 + [0, 0]) if l == 0 else [2, 3, 3, 0]
    steps = []
    for s in range(STEPS[l]):
        jobs = [ep[s]] if s < len(ep) else []
        jobs += st[:per[s]]
        st = st[per[s]:]
        steps.append(jobs)
    if kind != "last":
        steps[STEPS[l] - (2 if l == 0 else 1)].append(("M", 0))
    assert not st
    return steps


def build(nc, x_d, w_d, wo_d, cols_d, y_d):
    f32, f32r = mybir.dt.float32, mybir.dt.float32r
    ALU, ACT, AX = mybir.AluOpType, mybir.ActivationFunctionType, mybir.AxisListType
    ds = bass.ds

    x_v = x_d.rearrange("b (t p) n -> p (b t) n", p=P)
    y_v = y_d.rearrange("b (t p) n -> p (b t) n", p=P)
    w_v = w_d.rearrange("(t p) m -> p t m", p=P)

    ctx = ExitStack()
    with ctx:
        def sb(name, shape, dt=f32):
            return ctx.enter_context(nc.sbuf_tensor(name, shape, dt))

        def pb(name, shape):
            return ctx.enter_context(nc.psum_tensor(name, shape, f32))

        def sem(name):
            return ctx.enter_context(nc.semaphore(name))

        x_sb = sb("x_sb", [P, CT, N])
        keys = sb("keys", [P, N], f32r)
        queries = sb("queries", [P, N], f32r)
        q_ahead = sb("q_ahead", [R3, CH], f32r)
        vh = sb("vh", [P, KT[0], C], f32r)
        vl = sb("vl", [P, KT[0], C], f32r)
        gh = sb("gh", [P, KT[1], DV], f32r)
        gl = sb("gl", [P, KT[1], DV], f32r)
        prob_sb = sb("prob", [P, 2, 2, CH])
        prob = [prob_sb[:, i, :, :] for i in range(2)]
        prob_h = [sb(f"prob_h{i}", [P, 2, CH], f32r) for i in range(2)]
        prob_l = [sb(f"prob_l{i}", [P, 2, CH], f32r) for i in range(2)]
        xh = [sb(f"xh{i}", [P, CT, CH], f32r) for i in range(2)]
        xl = [sb(f"xl{i}", [P, CT, CH], f32r) for i in range(2)]
        w_sb = prob_sb[:, :, :, :].rearrange("p i t c -> p (i t c)")[:, 0:CT * WCOLS].rearrange(
            "p (t m) -> p t m", t=CT)
        wh = sb("wh", [P, CT, WCOLS], f32r)
        wl = sb("wl", [P, CT, WCOLS], f32r)
        wo = sb("wo", [DV, C])
        cols = sb("cols", [P, NCOLS])
        gbv = sb("gbv", [P, CT])
        cb = sb("cb", [P, CT])
        ident = sb("ident", [P, P])
        ident_r = sb("ident_r", [P, P], f32r)
        ones = sb("ones", [P, P])
        mx = sb("mx", [P, SUBS, NCH])
        nm = sb("nm", [P, SUBS])
        nm_wide = sb("nm_wide", [P, SUBS, P], f32r)
        psums = sb("psums", [P, CH])
        rsum = sb("rsum", [P, SUBS])
        rdiag = sb("rdiag", [P, CH])
        osb = sb("osb", [P, CT, CH])
        gpool = sb("gpool", [P, P])
        ppool = sb("ppool", [R3, P])

        s_ps = [pb(f"s_ps{i}", [P, 2, CH]) for i in range(2)]
        o_ps = [pb(f"o_ps{i}", [P, CH]) for i in range(2)]
        aux = pb("aux", [P, CH])
        acc = pb("acc", [P, CH])
        pj = [s_ps[0][:, 0, :], s_ps[0][:, 1, :], s_ps[1][:, 0, :], s_ps[1][:, 1, :]]

        w_in, cols_in = sem("w_in"), sem("cols_in")
        x_in = [sem("x_in0"), sem("x_in1")]
        y_out = [sem("y_out0"), sem("y_out1")]
        ident_ready, consts_ready, w_ready, dve_setup = (
            sem("ident_ready"), sem("consts_ready"), sem("w_ready"), sem("dve_setup"))
        x_split = sem("x_split")
        pj_full = sem("pj_full")
        pj_drained = sem("pj_drained")
        hi_ready = sem("hi_ready")
        q_ahead_ready = sem("q_ahead_ready")
        s_full = sem("s_full")
        p_ready = sem("p_ready")
        ph_ready = sem("ph_ready")
        pl_ready = sem("pl_ready")
        av_h = sem("av_h")
        av_l = sem("av_l")
        acc_done = sem("acc_done")
        aux_full = sem("aux_full")
        aux_free = sem("aux_free")
        mx_chain = sem("mx_chain")
        nm_ready = sem("nm_ready")
        psums_ready = sem("psums_ready")
        rdiag_ready = sem("rdiag_ready")
        o_act, o_dve = sem("o_act"), sem("o_dve")
        norm_done = sem("norm_done")
        x1_ready = sem("x1_ready")
        y_ready = sem("y_ready")

        def chunk(n):
            return ds(n * CH, CH)

        def attend_loop(eng, l, body):
            body(0, "first")
            with eng.Fori(1, NCH - DIST[l]) as n:
                body(n, "mid")
            for n in range(NCH - DIST[l], NCH):
                body(n, "last")

        def first_jobs(l, b, n, kind):
            base, k, out = aux_base(l, b, n), 0, []
            for jobs in schedule(l, kind):
                out.append([(base + (k + i), name, arg) for i, (name, arg) in enumerate(jobs)])
                k += len(jobs)
            return out

        block = ctx.enter_context(nc.Block())

        @block.sync
        def _(sp):
            def load_x(b, c, par, before):
                if before is not None:
                    sp.wait_ge(x_in[par], before)
                sp.dma_start(x_sb[:, :, chunk(c)], x_v[:, ds(b * CT, CT), chunk(c)]).then_inc(x_in[par], 16)

            for c in range(NCH):
                load_x(0, c, c % 2, 16 * (c // 2) if c >= 2 else None)

            def store_y(b, c, par):
                sp.wait_ge(y_ready, (b * NCH + c) * CT + CT)
                sp.dma_start(y_v[:, ds(b * CT, CT), chunk(c)], x_sb[:, :, chunk(c)]).then_inc(y_out[par], 16)

            with sp.Fori(0, B - 1) as b:
                for c in range(NCH):
                    par, k = c % 2, c // 2
                    store_y(b, c, par)
                    stored = sp.snap(sp.to_reg(b * (16 * NCH // 2) + 16 * (k + 1)))
                    before = sp.snap(sp.to_reg(b * (16 * NCH // 2) + 16 * (NCH // 2 + k)))
                    sp.wait_ge(y_out[par], stored)
                    load_x(b + 1, c, par, before)
            for c in range(NCH):
                store_y(B - 1, c, c % 2)
            for par in range(2):
                sp.wait_ge(y_out[par], 16 * B * NCH // 2)

        @block.gpsimd
        def _(pool):
            nc.gpsimd.memset(ident[:, :], 0.0).then_inc(ident_ready, 1)
            nc.gpsimd.memset(ones[:, :], 1.0)
            nc.gpsimd.memset(nm_wide[:, :, :].bitcast(f32), 0.0)
            pool.wait_ge(ident_ready, 1)
            nc.gpsimd.affine_select(out=ident[:, :], in_=ident[:, :], compare_op=ALU.not_equal, fill=1.0,
                                    base=0, pattern=[[-1, P]], channel_multiplier=1).then_inc(consts_ready, 1)

            def wait_alone(sem_, value):
                value = pool.snap(pool.to_reg(value))
                pool.wait_ge(consts_ready, 1)
                pool.wait_ge(sem_, value)

            def split_x(l, b, c, par):
                pc = chunk_no(l, b, c)
                if l == 0:
                    pool.wait_ge(x_in[par], b * (16 * NCH // 2) + (c - par) * 8 + 16)
                else:
                    pool.wait_ge(x1_ready, b * NCH + c + 1)
                wait_alone(pj_full, CREDIT - 4 + 4 * pc)
                nc.gpsimd.tensor_copy(xh[par][:, :, :], x_sb[:, :, chunk(c)]).then_inc(x_split, 1)
                wait_alone(x_split, 2 * pc + 1)
                nc.gpsimd.tensor_tensor(out=xl[par][:, :, :], in0=x_sb[:, :, chunk(c)],
                                        in1=xh[par][:, :, :].bitcast(f32), op=ALU.subtract).then_inc(x_split, 1)

            def copy_q_ahead(n):
                return nc.gpsimd.tensor_copy(q_ahead[:, :], queries[0:R3, chunk(n)].bitcast(f32))

            def split_prob(g, wait_buffer):
                pool.wait_ge(ph_ready, g + 1)
                if wait_buffer:
                    pool.wait_ge(av_l, g - 1)
                i = par_of[0]
                nc.gpsimd.tensor_tensor(out=prob_l[i][:, :, :], in0=prob[i],
                                        in1=prob_h[i][:, :, :].bitcast(f32), op=ALU.subtract).then_inc(pl_ready, 1)

            par_of = [0]

            def attend(l, b):
                def body(n, kind):
                    if kind != "last":
                        wait_alone(aux_full, aux_base(l, b, n))
                        copy_q_ahead(n + DIST[l]).then_inc(q_ahead_ready, 1)
                    for s in range(STEPS[l]):
                        par_of[0] = s % 2
                        split_prob(step_no(l, b, n, s), kind != "first" or s >= 2)
                attend_loop(pool, l, body)

            with pool.Fori(0, B) as b:
                split_x(0, b, 0, 0)
                split_x(0, b, 1, 1)
                wait_alone(pj_drained, CREDIT + 4 * chunk_no(0, b, 0) + 2)
                copy_q_ahead(0).then_inc(q_ahead_ready, 1)
                with pool.Fori(1, NCH // 2) as cc:
                    for par in range(2):
                        split_x(0, b, cc * 2 + par, par)
                attend(0, b)
                with pool.Fori(0, NCH // 2) as cc:
                    for par in range(2):
                        split_x(1, b, cc * 2 + par, par)
                for n in range(DIST[1]):
                    if n == 0:
                        wait_alone(pj_drained, CREDIT + 4 * chunk_no(1, b, NCH))
                    else:
                        wait_alone(aux_full, aux_base(1, b, 0) - DIST[1] * (NST[1] + 1) + n * (NST[1] + 1))
                    copy_q_ahead(n).then_inc(q_ahead_ready, 1)
                attend(1, b)

        @block.scalar
        def _(act):
            act.dma_start(w_sb, w_v).then_inc(w_in, 16)
            act.dma_start(wo[:, :], wo_d).then_inc(cols_in, 16)
            act.dma_start(cols[:, :], cols_d).then_inc(cols_in, 16)
            act.wait_ge(cols_in, 32)
            nc.scalar.activation(gbv[:, :], cols[:, COL_BV:COL_BV + CT], ACT.Copy,
                                 scale=cols[:, COL_G0:COL_G0 + 1]).then_inc(o_act, O_CREDIT)

            def high(l, b, c):
                pc = chunk_no(l, b, c)

                def full(k):
                    act.wait_ge(pj_full, CREDIT + 4 * pc + (k + 1))

                def biased(dst, src, col):
                    nc.scalar.activation(dst, src, ACT.Identity, bias=cols[0:R3, col:col + 1]).then_inc(hi_ready, 1)

                if l == 0:
                    full(0)
                    biased(keys[0:R3, chunk(c)], pj[0][0:R3, :], COL_BQ)
                    full(1)
                    biased(queries[0:R3, chunk(c)], pj[1][0:R3, :], COL_BK)
                    for k in (2, 3):
                        full(k)
                        nc.scalar.activation(vh[:, ds(c * SUBS + 2 * (k - 2), 2), :],
                                             pj[k].rearrange("p (t m) -> p t m", t=2), ACT.Copy).then_inc(hi_ready, 1)
                else:
                    act.wait_ge(pj_drained, CREDIT + 4 * pc + 2)
                    biased(keys[0:R3, ds(c * P, P)], ppool[:, :], COL_BPHI)
                    full(2)
                    biased(queries[0:R3, chunk(c)], pj[1][0:R3, :], COL_BTH)
                    full(3)
                    nc.scalar.activation(gh[:, ds(c, 1), :].rearrange("p t m -> p (t m)"), pj[3][:, 0:P],
                                         ACT.Copy).then_inc(hi_ready, 1)

            def exps(g, i, wait_buffers):
                act.wait_ge(s_full, g + 1)
                if wait_buffers:
                    act.wait_ge(pl_ready, g - 1)
                    act.wait_ge(acc_done, 2 * g - 2)
                nc.scalar.activation(prob[i], s_ps[i][:, :, :], ACT.Exp).then_inc(p_ready, 1)
                if wait_buffers:
                    act.wait_ge(av_h, g - 1)
                nc.scalar.activation(prob_h[i][:, :, :], s_ps[i][:, :, :], ACT.Exp).then_inc(ph_ready, 1)

            def copy_o(l, b, n):
                act.wait_ge(av_l, step_no(l, b, n, 0))
                act.wait_ge(aux_free, AUX_CREDIT + aux_base(l, b, n))
                nc.scalar.activation(osb[:, 0, :], o_ps[0][:, :], ACT.Copy).then_inc(o_act, 1)

            def add_cb(b, n, a0):
                for ct in range(CT):
                    act.wait_ge(aux_free, AUX_CREDIT + a0 + (ct + 1))
                    nc.scalar.activation(x_sb[:, ct, chunk(n - 1)], x_sb[:, ct, chunk(n - 1)], ACT.Identity,
                                         bias=cb[:, ct:ct + 1]).then_inc(y_ready, 1)

            def attend(l, b):
                def body(n, kind):
                    jobs = first_jobs(l, b, n, kind)
                    for s in range(STEPS[l]):
                        if s == 1 and kind != "first":
                            copy_o(l, b, n)
                        exps(step_no(l, b, n, s), s % 2, kind != "first" or s >= 2)
                        for a, name, ct in jobs[s]:
                            if name == "Z":
                                act.wait_ge(aux_free, AUX_CREDIT + a + 1)
                                nc.scalar.activation(x_sb[:, ct, chunk(n - 1)], x_sb[:, ct, chunk(n - 1)],
                                                     ACT.Identity, bias=cb[:, ct:ct + 1]).then_inc(y_ready, 1)
                attend_loop(act, l, body)
                copy_o(l, b, NCH)
                if l == 1:
                    add_cb(b, NCH, aux_base(l, b, NCH) + 2)

            act.wait_ge(pj_drained, CREDIT)
            with act.Fori(0, B) as b:
                for l in range(2):
                    with act.Fori(0, NCH) as c:
                        high(l, b, c)
                    attend(l, b)

        @block.vector
        def _(dve):
            nc.vector.memset(keys[R3:P, :].bitcast(f32), 1.0).then_inc(aux_free, AUX_CREDIT)
            dve.wait_ge(w_in, 16)
            nc.vector.tensor_copy(wh[:, :, :], w_sb).then_inc(dve_setup, 1)
            dve.wait_ge(dve_setup, 1)
            nc.vector.tensor_tensor(out=wl[:, :, :], in0=w_sb, in1=wh[:, :, :].bitcast(f32),
                                    op=ALU.subtract).then_inc(w_ready, 1)
            dve.wait_ge(cols_in, 32)
            dve.wait_ge(consts_ready, 1)
            nc.vector.tensor_copy(ident_r[:, :], ident[:, :]).then_inc(o_dve, O_CREDIT)
            dve.wait_ge(pj_full, CREDIT)
            nc.vector.tensor_tensor(out=cb[:, :], in0=cols[:, COL_BO:COL_BO + CT], in1=aux[:, 0:CT],
                                    op=ALU.add).then_inc(dve_setup, 1)
            dve.wait_ge(dve_setup, 2)
            nc.vector.tensor_scalar(cb[:, :], cb[:, :], cols[:, COL_G1:COL_G1 + 1], None,
                                    ALU.mult).then_inc(pj_drained, CREDIT)

            def st_drain(a, sub, c):
                dve.wait_ge(aux_full, a + 1)
                nc.vector.tensor_reduce(out=mx[:, sub, c], in_=aux[:, :], axis=AX.X, op=ALU.max).then_inc(aux_free, 1)

            def finish_max(l, a, target):
                dve.wait_ge(aux_free, AUX_CREDIT + a + 1)
                nc.vector.tensor_reduce(out=nm[:, :], in_=mx[:, :, 0:KEYS[l] // CH], axis=AX.X, op=ALU.max,
                                        negate=True).then_inc(mx_chain, 1)
                dve.wait_ge(mx_chain, 2 * target + 1)
                nc.vector.tensor_copy(nm_wide[:, :, R3], nm[:, :]).then_inc(mx_chain, 1)
                dve.wait_ge(mx_chain, 2 * target + 2)
                nc.vector.tensor_tensor(out=nm_wide[:, :, R3 + 1], in0=nm[:, :], in1=nm_wide[:, :, R3].bitcast(f32),
                                        op=ALU.subtract).then_inc(nm_ready, 1)

            def m_drain(a, n):
                dve.wait_ge(aux_full, a + 1)
                nc.vector.tensor_copy(queries[R3:P, chunk(n)], aux[R3:P, :]).then_inc(aux_free, 1)

            def low(dst, src, scalar, hi):
                if scalar is None:
                    return nc.vector.tensor_tensor(out=dst, in0=src, in1=hi.bitcast(f32), op=ALU.subtract)
                return nc.vector.scalar_tensor_tensor(out=dst, in0=src, scalar=scalar, in1=hi.bitcast(f32),
                                                      op0=ALU.add, op1=ALU.subtract)

            LK = slice(2 * DK, R3)
            LQ = slice(DK, 2 * DK)

            def project0(b, c, st):
                pc = chunk_no(0, b, c)
                a = b * AUX_BATCH + (c - 1) * SUBS
                for k in range(4):
                    dve.wait_ge(hi_ready, hi_no(0, b, c, k) + 1)
                    if k == 0:
                        ins = low(keys[LK, chunk(c)], pj[0][LK, :], cols[LK, COL_BQ:COL_BQ + 1], keys[LK, chunk(c)])
                    elif k == 1:
                        ins = low(queries[LQ, chunk(c)], pj[1][LQ, :], cols[LQ, COL_BK:COL_BK + 1],
                                  queries[LQ, chunk(c)])
                    else:
                        tiles = ds(c * SUBS + 2 * (k - 2), 2)
                        ins = low(vl[:, tiles, :], pj[k].rearrange("p (t m) -> p t m", t=2), None, vh[:, tiles, :])
                    ins.then_inc(pj_drained, 1)
                    if st:
                        st_drain(a + k, k, ds(c - 1, 1))

            def pool_max(dst, src):
                return nc.vector.tensor_reduce(
                    out=dst.rearrange("p (h w) -> p h w", w=PW),
                    in_=src.rearrange("p (h a w b) -> p h w a b", a=2, b=2, w=PW), axis=AX.XY, op=ALU.max)

            def project1(b, c):
                pc = chunk_no(1, b, c)
                dve.wait_ge(pj_drained, CREDIT + 4 * pc)
                dve.wait_ge(pj_full, CREDIT + 4 * pc + 1)
                pool_max(gpool[:, :], pj[2]).then_inc(pj_drained, 1)
                dve.wait_ge(pj_full, CREDIT + 4 * pc + 2)
                pool_max(ppool[:, :], pj[0][0:R3, :]).then_inc(pj_drained, 1)
                dve.wait_ge(hi_ready, hi_no(1, b, c, 0) + 1)
                low(keys[LK, ds(c * P, P)], ppool[LK, :], cols[LK, COL_BPHI:COL_BPHI + 1], keys[LK, ds(c * P, P)])
                dve.wait_ge(hi_ready, hi_no(1, b, c, 1) + 1)
                low(queries[LQ, chunk(c)], pj[1][LQ, :], cols[LQ, COL_BTH:COL_BTH + 1],
                    queries[LQ, chunk(c)]).then_inc(pj_drained, 1)
                dve.wait_ge(hi_ready, hi_no(1, b, c, 2) + 1)
                low(gl[:, ds(c, 1), :].rearrange("p t m -> p (t m)"), pj[3][:, 0:P], None,
                    gh[:, ds(c, 1), :].rearrange("p t m -> p (t m)")).then_inc(pj_drained, 1)

            def add_probs(g, s):
                i = s % 2
                dve.wait_ge(p_ready, g + 1)
                if s == 0:
                    nc.vector.tensor_copy(acc[:, :], prob[i][:, 0, :]).then_inc(acc_done, 1)
                else:
                    dve.wait_ge(acc_done, 2 * g)
                    nc.vector.tensor_tensor(out=acc[:, :], in0=prob[i][:, 0, :], in1=acc[:, :],
                                            op=ALU.add).then_inc(acc_done, 1)
                dve.wait_ge(acc_done, 2 * g + 1)
                nc.vector.tensor_tensor(out=acc[:, :], in0=prob[i][:, 1, :], in1=acc[:, :],
                                        op=ALU.add).then_inc(acc_done, 1)

            def drain(l, b, n, a, name, arg):
                if name == "ST":
                    st_drain(a, arg % SUBS, slice(arg // SUBS, arg // SUBS + 1))
                    if arg == NST[l] - 1:
                        finish_max(l, a, chunk_no(l, b, n + DIST[l]))
                elif name == "M":
                    m_drain(a, n + DIST[l])
                elif name == "D1":
                    dve.wait_ge(aux_full, a + 1)
                    nc.vector.reciprocal(rsum[:, :], aux[:, 0:SUBS]).then_inc(aux_free, 1)
                    dve.wait_ge(aux_free, AUX_CREDIT + a + 1)
                    for s in range(SUBS):
                        last = nc.vector.tensor_scalar(rdiag[:, s * P:(s + 1) * P], ident[:, :], rsum[:, s:s + 1],
                                                       None, ALU.mult)
                    last.then_inc(rdiag_ready, 1)
                elif name == "D2":
                    dve.wait_ge(aux_full, a + 1)
                    dve.wait_ge(o_act, O_CREDIT + chunk_no(l, b, n))
                    if l == 0:
                        nc.vector.scalar_tensor_tensor(out=osb[:, 0, :], in0=osb[:, 0, :],
                                                       scalar=cols[:, COL_G0:COL_G0 + 1], in1=aux[:, :],
                                                       op0=ALU.mult, op1=ALU.mult).then_inc(norm_done, 1)
                        nc.vector.scalar_tensor_tensor(out=osb[:, 1, :], in0=osb[:, 1, :],
                                                       scalar=cols[:, COL_G0:COL_G0 + 1], in1=aux[:, :],
                                                       op0=ALU.mult, op1=ALU.mult).then_inc(aux_free, 1)
                        dve.wait_ge(norm_done, b * NCH + n)
                        nc.vector.scalar_tensor_tensor(
                            out=x_sb[:, 0, chunk(n - 1)], in0=osb[:, 0, :], scalar=gbv[:, 0:1],
                            in1=x_sb[:, 0, chunk(n - 1)], op0=ALU.add, op1=ALU.add)
                        dve.wait_ge(aux_free, AUX_CREDIT + a + 1)
                        nc.vector.scalar_tensor_tensor(
                            out=x_sb[:, 1, chunk(n - 1)], in0=osb[:, 1, :], scalar=gbv[:, 1:2],
                            in1=x_sb[:, 1, chunk(n - 1)], op0=ALU.add, op1=ALU.add).then_inc(x1_ready, 1)
                    else:
                        nc.vector.tensor_tensor(out=osb[:, 1, :], in0=osb[:, 0, :], in1=aux[:, :],
                                                op=ALU.mult).then_inc(aux_free, 1)
                elif name == "Z":
                    dve.wait_ge(aux_full, a + 1)
                    nc.vector.scalar_tensor_tensor(out=x_sb[:, arg, chunk(n - 1)], in0=aux[:, :],
                                                   scalar=cols[:, COL_G1:COL_G1 + 1], in1=x_sb[:, arg, chunk(n - 1)],
                                                   op0=ALU.mult, op1=ALU.add).then_inc(aux_free, 1)

            def copy_o(b, n):
                dve.wait_ge(av_l, step_no(0, b, n, 0))
                nc.vector.tensor_copy(osb[:, 1, :], o_ps[1][:, :]).then_inc(o_dve, 1)

            def attend(l, b):
                def body(n, kind):
                    jobs = first_jobs(l, b, n, kind)
                    if l == 0 and kind != "first":
                        copy_o(b, n)
                    for s in range(STEPS[l]):
                        g = step_no(l, b, n, s)
                        for a, name, arg in jobs[s][:1]:
                            drain(l, b, n, a, name, arg)
                        add_probs(g, s)
                        for a, name, arg in jobs[s][1:]:
                            drain(l, b, n, a, name, arg)
                    dve.wait_ge(acc_done, 2 * step_no(l, b, n, STEPS[l]))
                    nc.vector.tensor_copy(psums[:, :], acc[:, :]).then_inc(psums_ready, 1)
                attend_loop(dve, l, body)
                if l == 0:
                    copy_o(b, NCH)
                a = aux_base(l, b, NCH)
                for k, (name, arg) in enumerate([("D1", 0), ("D2", 0), ("Z", 0), ("Z", 1)][:NEP[l]]):
                    drain(l, b, NCH, a + k, name, arg)

            with dve.Fori(0, B) as b:
                project0(b, 0, False)
                with dve.Fori(1, NCH) as c:
                    project0(b, c, True)
                a = b * AUX_BATCH
                for k in range(SUBS):
                    st_drain(a + ((NCH - 1) * SUBS + k), k, slice(NCH - 1, NCH))
                finish_max(0, a + (NST[0] - 1), chunk_no(0, b, 0))
                m_drain(a + NST[0], 0)
                attend(0, b)
                with dve.Fori(0, NCH) as c:
                    project1(b, c)
                a = b * AUX_BATCH + NCH * AUX_CHUNK[0]
                for n in range(DIST[1]):
                    for k in range(NST[1]):
                        st_drain(a + (n * (NST[1] + 1) + k), k % SUBS, slice(k // SUBS, k // SUBS + 1))
                    finish_max(1, a + (n * (NST[1] + 1) + NST[1] - 1), chunk_no(1, b, n))
                    m_drain(a + (n * (NST[1] + 1) + NST[1]), n)
                attend(1, b)

        @block.tensor
        def _(pe):
            mm = nc.tensor.matmul
            pe.wait_ge(cols_in, 32)
            for ct in range(CT):
                last = mm(aux[:, ct:ct + 1], wo[:, ct * P:(ct + 1) * P], cols[:, COL_BG:COL_BG + 1],
                          start=True, stop=True)
            last.then_inc(pj_full, CREDIT)
            pe.wait_ge(w_ready, 1)
            pe.wait_ge(pj_drained, CREDIT)

            def st_job(a, sub, c):
                pe.wait_ge(aux_free, AUX_CREDIT + a)
                mm(aux[:, :], q_ahead[:, sub * P:(sub + 1) * P], keys[0:R3, chunk(c)],
                   start=True, stop=True).then_inc(aux_full, 1)

            def m_job(a, target):
                pe.wait_ge(aux_free, AUX_CREDIT + a)
                pe.wait_ge(nm_ready, target + 1)
                for s in range(SUBS):
                    last = mm(aux[:, s * P:(s + 1) * P], nm_wide[:, s, :], ident_r[:, :], start=True, stop=True)
                last.then_inc(aux_full, 1)

            def conv(dst, w0, width, par, wait):
                first = True
                for kt in range(CT):
                    for w in (wh, wl):
                        mm(dst, w[:, kt, w0:w0 + width], xh[par][:, kt, :], start=first, stop=False)
                        first = False
                if wait is not None:
                    pe.wait_ge(x_split, wait)
                for kt in range(CT):
                    last = mm(dst, wh[:, kt, w0:w0 + width], xl[par][:, kt, :], start=False, stop=kt == CT - 1)
                return last

            def project0(b, c, par, st):
                pc = chunk_no(0, b, c)
                a = b * AUX_BATCH + (c - 1) * SUBS
                for k in range(4):
                    pe.wait_ge(pj_drained, CREDIT - 4 + 4 * pc + (k + 1))
                    if k == 0:
                        pe.wait_ge(x_split, 2 * pc + 1)
                        last = conv(pj[0][0:R3, :], W_Q, R3, par, 2 * pc + 2)
                    elif k == 1:
                        last = conv(pj[1][0:R3, :], W_K, R3, par, None)
                    else:
                        for t in range(2):
                            pos = slice((2 * (k - 2) + t) * P, (2 * (k - 2) + t + 1) * P)
                            dst = pj[k][:, t * C:(t + 1) * C]
                            first = True
                            for kt in range(CT):
                                for w in (wh, wl):
                                    mm(dst, xh[par][:, kt, pos], w[:, kt, W_V:W_V + C], start=first, stop=False)
                                    first = False
                            for kt in range(CT):
                                last = mm(dst, xl[par][:, kt, pos], wh[:, kt, W_V:W_V + C], start=False,
                                          stop=kt == CT - 1)
                    last.then_inc(pj_full, 1)
                    if st:
                        if k == 0:
                            pe.wait_ge(q_ahead_ready, chunk_no(0, b, 0) + 1)
                        st_job(a + k, k, c - 1)

            def project1(b, c, par):
                pc = chunk_no(1, b, c)
                for k, (bank, w0, width) in enumerate(((2, W_G, DV), (0, W_PHI, R3), (1, W_TH, R3))):
                    pe.wait_ge(pj_drained, CREDIT - 4 + 4 * pc + (k + 1))
                    if k == 0:
                        pe.wait_ge(x_split, 2 * pc + 1)
                    conv(pj[bank][0:width, :], w0, width, par, 2 * pc + 2 if k == 0 else None).then_inc(pj_full, 1)
                pe.wait_ge(pj_drained, CREDIT + 4 * pc)
                pe.wait_ge(pj_drained, CREDIT + 4 * pc + 1)
                nc.tensor.transpose(pj[3][:, 0:P], gpool[:, :], ident[:, :]).then_inc(pj_full, 1)

            def scores(l, n, s):
                i = s % 2
                for t in range(2):
                    kt = 2 * s + t
                    last = mm(s_ps[i][:, t, :], keys[:, kt * P:(kt + 1) * P], queries[:, chunk(n)],
                              start=True, stop=True)
                last.then_inc(s_full, 1)

            def av(l, s, low):
                i = s % 2
                hi_t, lo_t = (vh, vl) if l == 0 else (gh, gl)
                for t in range(2):
                    kt = 2 * s + t
                    for ct in range(VT[l]):
                        cols_ = slice(ct * P, (ct + 1) * P)
                        if low:
                            last = mm(o_ps[ct][:, :], hi_t[:, kt, cols_], prob_l[i][:, t, :], start=False,
                                      stop=kt == KT[l] - 1)
                        else:
                            mm(o_ps[ct][:, :], hi_t[:, kt, cols_], prob_h[i][:, t, :], start=kt == 0, stop=False)
                            last = mm(o_ps[ct][:, :], lo_t[:, kt, cols_], prob_h[i][:, t, :], start=False, stop=False)
                last.then_inc(av_l if low else av_h, 1)

            def job(l, b, n, a, name, arg):
                if name == "ST":
                    if arg == 0:
                        pe.wait_ge(q_ahead_ready, chunk_no(l, b, n + DIST[l]) + 1)
                    st_job(a, arg % SUBS, arg // SUBS)
                elif name == "M":
                    m_job(a, chunk_no(l, b, n + DIST[l]))
                elif name == "D1":
                    pe.wait_ge(aux_free, AUX_CREDIT + a)
                    pe.wait_ge(psums_ready, chunk_no(l, b, n))
                    for s in range(SUBS):
                        last = mm(aux[:, s:s + 1], psums[:, s * P:(s + 1) * P], ones[:, 0:1], start=True, stop=True)
                    last.then_inc(aux_full, 1)
                elif name == "D2":
                    pe.wait_ge(aux_free, AUX_CREDIT + a)
                    pe.wait_ge(rdiag_ready, chunk_no(l, b, n))
                    mm(aux[:, :], ones[:, :], rdiag[:, :], start=True, stop=True).then_inc(aux_full, 1)
                elif name == "Z":
                    pe.wait_ge(aux_free, AUX_CREDIT + a)
                    mm(aux[:, :], wo[:, arg * P:(arg + 1) * P], osb[:, 1, :], start=True,
                       stop=True).then_inc(aux_full, 1)

            def attend(l, b):
                def body(n, kind):
                    jobs = first_jobs(l, b, n, kind)
                    for s in range(STEPS[l]):
                        g = step_no(l, b, n, s)
                        if s + 1 < STEPS[l]:
                            scores(l, n, s + 1)
                        elif not (isinstance(n, int) and n == NCH - 1):
                            pe.wait_ge(aux_free, AUX_CREDIT + (aux_base(l, b, n + 1) if l == 0 else aux_base(l, b, n)))
                            scores(l, n + 1, 0)
                        for j in jobs[s][:1]:
                            job(l, b, n, *j)
                        if s:
                            pe.wait_ge(pl_ready, g)
                            av(l, s - 1, True)
                        for j in jobs[s][1:2]:
                            job(l, b, n, *j)
                        if s == 0:
                            pe.wait_ge(o_act, O_CREDIT + chunk_no(l, b, n))
                            if l == 0:
                                pe.wait_ge(o_dve, O_CREDIT + b * NCH + n)
                        pe.wait_ge(ph_ready, g + 1)
                        av(l, s, False)
                        for j in jobs[s][2:]:
                            job(l, b, n, *j)
                    pe.wait_ge(pl_ready, step_no(l, b, n, STEPS[l]))
                    av(l, STEPS[l] - 1, True)

                pe.wait_ge(pj_drained, CREDIT + 4 * chunk_no(l, b, NCH))
                pe.wait_ge(aux_free, AUX_CREDIT + aux_base(l, b, 0))
                scores(l, 0, 0)
                attend_loop(pe, l, body)
                a = aux_base(l, b, NCH)
                for k, (name, arg) in enumerate([("D1", 0), ("D2", 0), ("Z", 0), ("Z", 1)][:NEP[l]]):
                    job(l, b, NCH, a + k, name, arg)

            with pe.Fori(0, B) as b:
                project0(b, 0, 0, False)
                project0(b, 1, 1, True)
                with pe.Fori(1, NCH // 2) as cc:
                    for par in range(2):
                        project0(b, cc * 2 + par, par, True)
                pe.wait_ge(pj_drained, CREDIT + 4 * chunk_no(0, b, NCH))
                a = b * AUX_BATCH
                for k in range(SUBS):
                    st_job(a + ((NCH - 1) * SUBS + k), k, NCH - 1)
                m_job(a + NST[0], chunk_no(0, b, 0))
                attend(0, b)
                with pe.Fori(0, NCH // 2) as cc:
                    for par in range(2):
                        project1(b, cc * 2 + par, par)
                a = b * AUX_BATCH + NCH * AUX_CHUNK[0]
                for n in range(DIST[1]):
                    pe.wait_ge(q_ahead_ready, chunk_no(1, b, n) + 1)
                    for k in range(NST[1]):
                        st_job(a + (n * (NST[1] + 1) + k), k % SUBS, k // SUBS)
                    m_job(a + (n * (NST[1] + 1) + NST[1]), chunk_no(1, b, n))
                attend(1, b)


def kernel(x, L0_conv_Wq, L0_conv_bq, L0_conv_Wk, L0_conv_bk, L0_conv_Wv, L0_conv_bv, L0_conv_gamma,
           L1_conv_theta_w, L1_conv_theta_b, L1_conv_phi_w, L1_conv_phi_b, L1_conv_g_w, L1_conv_g_b,
           L1_conv_out_w, L1_conv_out_b, L1_conv_gamma):
    import numpy as np
    import concourse.bacc as bacc
    from concourse.bass_utils import run_bass_kernel_spmd

    def thrice(w):
        return np.concatenate([np.asarray(w).T] * 3, axis=1)

    w = np.concatenate([thrice(L0_conv_Wq), thrice(L0_conv_Wk), np.asarray(L0_conv_Wv).T, thrice(L1_conv_phi_w),
                        thrice(L1_conv_theta_w), np.asarray(L1_conv_g_w).T], axis=1)
    cols = np.zeros((P, NCOLS), np.float32)
    for col, v in ((COL_BQ, L0_conv_bq), (COL_BK, L0_conv_bk), (COL_BPHI, L1_conv_phi_b), (COL_BTH, L1_conv_theta_b)):
        cols[:R3, col] = np.concatenate([np.asarray(v)] * 3)
    cols[:, COL_BV:COL_BV + CT] = np.asarray(L0_conv_bv).reshape(CT, P).T
    cols[:, COL_BG] = np.asarray(L1_conv_g_b)
    cols[:, COL_BO:COL_BO + CT] = np.asarray(L1_conv_out_b).reshape(CT, P).T
    cols[:, COL_G0] = np.broadcast_to(np.asarray(L0_conv_gamma), (P,))
    cols[:, COL_G1] = np.broadcast_to(np.asarray(L1_conv_gamma), (P,))
    arrays = {
        "x": np.ascontiguousarray(np.asarray(x).reshape(B, C, N)),
        "w_in": np.ascontiguousarray(w),
        "w_out": np.ascontiguousarray(np.asarray(L1_conv_out_w).T),
        "columns": cols,
    }
    f32 = mybir.dt.float32
    nc = bacc.Bacc("TRN2", target_bir_lowering=False, num_devices=1)
    ins = [nc.dram_tensor(k, a.shape, f32, kind="ExternalInput").ap() for k, a in arrays.items()]
    y = nc.dram_tensor("y", (B, C, N), f32, kind="ExternalOutput").ap()
    build(nc, *ins, y)
    r = run_bass_kernel_spmd(nc, [arrays], core_ids=[0])
    return r.results[0]["y"].reshape(B, C, IMG_W, IMG_W)
```

```python
from contextlib import ExitStack

import concourse.bass as bass
from concourse import mybir

B, C, N = 4, 256, 4096
P = 128
DK = C // 8
DV = C // 2
CT = C // P
R3 = 3 * DK
CH = 512
NCH = N // CH
SUBS = CH // P
IMG_W = 64
PW = IMG_W // 2
CHROWS = CH // IMG_W
KEYS = (N, N // 4)
KT = tuple(k // P for k in KEYS)
STEPS = tuple(t // 2 for t in KT)
DIST = (1, 2)
VT = (CT, 1)
NST = tuple(SUBS * k // CH for k in KEYS)
STS = ((NST[0], 0), (NST[1] // 2, NST[1] // 2))
MS = (1, 0)
EPS = ((2, 0), (2, 2))
WCOLS = 4 * R3 + C + DV
W_Q, W_K, W_V, W_PHI, W_TH, W_G = 0, R3, 2 * R3, 2 * R3 + C, 3 * R3 + C, 4 * R3 + C
COL_BQ, COL_BK, COL_BPHI, COL_BTH, COL_BV, COL_BG, COL_BO, COL_G0, COL_G1 = 0, 1, 2, 3, 4, 6, 7, 9, 10
NCOLS = 11

STEP_BATCH = NCH * sum(STEPS)
CHUNK_BATCH = 2 * NCH
AUX_CHUNK = tuple(tuple(STS[l][k] + MS[k] + EPS[l][k] for k in range(2)) for l in range(2))
AUX_BATCH = tuple(NCH * (AUX_CHUNK[0][k] + AUX_CHUNK[1][k]) for k in range(2))
HI_CHUNK = (4, 3)
HI_BATCH = NCH * sum(HI_CHUNK)
CREDIT = 8
ONE = 1


def step_no(l, b, n, s):
    return b * STEP_BATCH + (l * NCH * STEPS[0] + s) + n * STEPS[l]


def chunk_no(l, b, n):
    return b * CHUNK_BATCH + n + l * NCH


def aux_base(l, b, n, k=0):
    off = l * NCH * AUX_CHUNK[0][k] + DIST[l] * (STS[l][k] + MS[k])
    if isinstance(n, int) and n == 0:
        return b * AUX_BATCH[k] + off
    off += STS[l][k] + MS[k]
    full = NCH - 1 - DIST[l]
    if isinstance(n, int) and n > full + 1:
        return b * AUX_BATCH[k] + (off + full * AUX_CHUNK[l][k] + (n - 1 - full) * EPS[l][k])
    return b * AUX_BATCH[k] + off + (n - 1) * AUX_CHUNK[l][k]


def aux_start(l, b, k=0):
    return b * AUX_BATCH[k] + l * NCH * AUX_CHUNK[0][k]


def bank_of(l, name, arg):
    return {"ST": arg % 2, "M": 0, "D1": 1, "D2": 0, "Z": 1 - arg}[name] if l else 0


def hi_no(l, b, c, k):
    return b * HI_BATCH + (l * NCH * HI_CHUNK[0] + k) + c * HI_CHUNK[l]


ST_STEPS = ([1, 2, 2, 3, 2, 3, 2, 3, 2, 3, 2, 3, 2, 2, 0, 0], [3, 3, 2, 0])
EP_STEPS = ({"D1": 0, "D2": 2}, {"D1": 0, "D2": 1, "Z0": 3, "Z1": 3})
M_STEP = (14, 3)
NORM_STEPS = ((3, 4, 5, 6), (2,))


def schedule(l, kind):
    steps, k = [], 0
    for s in range(STEPS[l]):
        jobs = []
        if kind != "first":
            jobs += [(e[0] if e[0] == "Z" else e, int(e[1]) if e[0] == "Z" else 0)
                     for e, at in EP_STEPS[l].items() if at == s]
        if kind != "last":
            jobs += [("ST", k + i) for i in range(ST_STEPS[l][s])]
            k += ST_STEPS[l][s]
            if s == M_STEP[l]:
                jobs.insert(1 if l else 0, ("M", 0))
        steps.append(jobs)
    assert k == (0 if kind == "last" else NST[l])
    return steps


def tail_jobs(l):
    return [("D1", 0), ("D2", 0), ("Z", 0), ("Z", 1)][:4 if l else 2]


def build(nc, x_d, w_d, wo_d, cols_d, y_d):
    f32, f32r = mybir.dt.float32, mybir.dt.float32r
    ALU, ACT, AX = mybir.AluOpType, mybir.ActivationFunctionType, mybir.AxisListType
    ds = bass.ds

    x_v = x_d.rearrange("b (t p) n -> p (b t) n", p=P)
    y_v = y_d.rearrange("b (t p) n -> p (b t) n", p=P)
    w_v = w_d.rearrange("(t p) m -> p t m", p=P)

    ctx = ExitStack()
    with ctx:
        def sb(name, shape, dt=f32):
            return ctx.enter_context(nc.sbuf_tensor(name, shape, dt))

        def pb(name, shape):
            return ctx.enter_context(nc.psum_tensor(name, shape, f32))

        def sem(name):
            return ctx.enter_context(nc.semaphore(name))

        x_sb = sb("x_sb", [P, CT, N])
        keys = sb("keys", [P, N], f32r)
        queries = sb("queries", [P, N], f32r)
        q_ahead = sb("q_ahead", [R3, CH], f32r)
        vh = sb("vh", [P, KT[0], C], f32r)
        vl = sb("vl", [P, KT[0], C], f32r)
        vh_flat = vh[:, :, :].rearrange("p t m -> p (t m)")
        vl_flat = vl[:, :, :].rearrange("p t m -> p (t m)")
        prob_sb = sb("prob", [P, 2, 2, CH])
        prob = [prob_sb[:, i, :, :] for i in range(2)]
        prob_h = [sb(f"prob_h{i}", [P, 2, CH], f32r) for i in range(2)]
        prob_l = [sb(f"prob_l{i}", [P, 2, CH], f32r) for i in range(2)]
        xh = [sb(f"xh{i}", [P, CT, CH], f32r) for i in range(2)]
        xl = [sb(f"xl{i}", [P, CT, CH], f32r) for i in range(2)]
        w_sb = prob_sb[:, :, :, :].rearrange("p i t c -> p (i t c)")[:, 0:CT * WCOLS].rearrange(
            "p (t m) -> p t m", t=CT)
        wh = sb("wh", [P, CT, WCOLS], f32r)
        wl = sb("wl", [P, CT, WCOLS], f32r)
        wo = sb("wo", [DV, C])
        cols = sb("cols", [P, NCOLS])
        gbv = sb("gbv", [P, CT])
        cb = sb("cb", [P, CT])
        ident = sb("ident", [P, P])
        ident_r = sb("ident_r", [P, P], f32r)
        ones = sb("ones", [P, P])
        mx = sb("mx", [P, SUBS, NCH])
        nm = sb("nm", [P, SUBS])
        nm_wide = sb("nm_wide", [P, SUBS, P], f32r)
        psums = sb("psums", [P, CH])
        rsum = sb("rsum", [P, SUBS])
        rdiag = sb("rdiag", [P, CH])
        rb = sb("rb", [P, CH])
        osb = sb("osb", [P, CT, CH])
        zc = sb("zc", [P, CH])
        gpool = sb("gpool", [P, P])
        ppool = sb("ppool", [R3, P])

        s_ps = [pb(f"s_ps{i}", [P, 2, CH]) for i in range(2)]
        o_ps = [pb(f"o_ps{i}", [P, CH]) for i in range(2)]
        aux = pb("aux", [P, CH])
        aux_bank = (aux, o_ps[1])
        acc = pb("acc", [P, CH])
        pj = [s_ps[0][:, 0, :], s_ps[0][:, 1, :], s_ps[1][:, 0, :], s_ps[1][:, 1, :]]

        w_in, cols_in = sem("w_in"), sem("cols_in")
        x_in = [sem("x_in0"), sem("x_in1")]
        y_out = [sem("y_out0"), sem("y_out1")]
        ident_ready, consts_ready, w_ready, dve_setup = (
            sem("ident_ready"), sem("consts_ready"), sem("w_ready"), sem("dve_setup"))
        xh_ready = sem("xh_ready")
        xl_ready = sem("xl_ready")
        pj_full = sem("pj_full")
        pj_drained = sem("pj_drained")
        hi_ready = sem("hi_ready")
        q_ahead_ready = sem("q_ahead_ready")
        s_full = sem("s_full")
        p_ready = sem("p_ready")
        ph_ready = sem("ph_ready")
        pl_ready = sem("pl_ready")
        av_h = sem("av_h")
        av_l = sem("av_l")
        acc_done = sem("acc_done")
        aux_full = [sem("aux_full0"), sem("aux_full1")]
        aux_free = [sem("aux_free0"), sem("aux_free1")]
        mx_chain = sem("mx_chain")
        nm_ready = sem("nm_ready")
        psums_ready = sem("psums_ready")
        rdiag_ready = sem("rdiag_ready")
        o_act, o_dve = sem("o_act"), sem("o_dve")
        norm_done = sem("norm_done")
        x1_ready = sem("x1_ready")
        y_ready = sem("y_ready")

        def chunk(n):
            return ds(n * CH, CH)

        def attend_loop(eng, l, body):
            body(0, "first")
            with eng.Fori(1, NCH - DIST[l]) as n:
                body(n, "mid")
            for n in range(NCH - DIST[l], NCH):
                body(n, "last")

        def body_jobs(l, b, n, kind):
            k, out = [0, 0], []
            for jobs in schedule(l, kind):
                out.append([])
                for name, arg in jobs:
                    bank = bank_of(l, name, arg)
                    out[-1].append((aux_base(l, b, n, bank) + k[bank], bank, name, arg))
                    k[bank] += 1
            return out

        def after_last(l, b):
            k, out = [0, 0], []
            for name, arg in tail_jobs(l):
                bank = bank_of(l, name, arg)
                out.append((aux_base(l, b, NCH, bank) + k[bank], bank, name, arg))
                k[bank] += 1
            return out

        def prologue_jobs(l, b, n):
            k, out = [0, 0], []
            for name, arg in [("ST", i) for i in range(NST[l])] + [("M", 0)]:
                bank = bank_of(l, name, arg)
                out.append((aux_start(l, b, bank) + (n * (STS[l][bank] + MS[bank]) + k[bank]), bank, name, arg))
                k[bank] += 1
            return out

        block = ctx.enter_context(nc.Block())

        @block.sync
        def _(sp):
            def load_x(b, c, par, before):
                if before is not None:
                    sp.wait_ge(x_in[par], before)
                sp.dma_start(x_sb[:, :, chunk(c)], x_v[:, ds(b * CT, CT), chunk(c)]).then_inc(x_in[par], 16)

            for c in range(NCH):
                load_x(0, c, c % 2, 16 * (c // 2) if c >= 2 else None)

            def store_y(b, c, par):
                sp.wait_ge(y_ready, ONE + (b * NCH + c) * CT + CT)
                sp.dma_start(y_v[:, ds(b * CT, CT), chunk(c)], x_sb[:, :, chunk(c)]).then_inc(y_out[par], 16)

            with sp.Fori(0, B - 1) as b:
                for c in range(NCH):
                    par, k = c % 2, c // 2
                    store_y(b, c, par)
                    stored = sp.snap(sp.to_reg(b * (16 * NCH // 2) + 16 * (k + 1)))
                    before = sp.snap(sp.to_reg(b * (16 * NCH // 2) + 16 * (NCH // 2 + k)))
                    sp.wait_ge(y_out[par], stored)
                    load_x(b + 1, c, par, before)
            for c in range(NCH):
                store_y(B - 1, c, c % 2)
            for par in range(2):
                sp.wait_ge(y_out[par], 16 * B * NCH // 2)

        @block.gpsimd
        def _(pool):
            nc.gpsimd.memset(ident[:, :], 0.0).then_inc(ident_ready, 1)
            nc.gpsimd.memset(ones[:, :], 1.0).then_inc(y_ready, ONE)
            nc.gpsimd.memset(nm_wide[:, :, :].bitcast(f32), 0.0)
            pool.wait_ge(ident_ready, 1)
            nc.gpsimd.affine_select(out=ident[:, :], in_=ident[:, :], compare_op=ALU.not_equal, fill=1.0,
                                    base=0, pattern=[[-1, P]], channel_multiplier=1).then_inc(consts_ready, 1)

            def wait_alone(sem_, value):
                value = pool.snap(pool.to_reg(value))
                pool.wait_ge(consts_ready, 1)
                pool.wait_ge(sem_, value)

            def split_x(l, b, c, par):
                wait_alone(xh_ready, chunk_no(l, b, c) + 1)
                nc.gpsimd.tensor_tensor(out=xl[par][:, :, :], in0=x_sb[:, :, chunk(c)],
                                        in1=xh[par][:, :, :].bitcast(f32), op=ALU.subtract).then_inc(xl_ready, 1)

            def split_prob(g, i, wait_buffer):
                pool.wait_ge(ph_ready, g + 1)
                if wait_buffer:
                    pool.wait_ge(av_l, g - 1)
                nc.gpsimd.tensor_tensor(out=prob_l[i][:, :, :], in0=prob[i],
                                        in1=prob_h[i][:, :, :].bitcast(f32), op=ALU.subtract).then_inc(pl_ready, 1)

            def add_x(b, n, a, bank, ct):
                wait_alone(aux_free[bank], ONE + a + 1)
                nc.gpsimd.tensor_tensor(out=x_sb[:, ct, chunk(n - 1)], in0=zc[:, :], in1=x_sb[:, ct, chunk(n - 1)],
                                        op=ALU.add).then_inc(y_ready, 1)

            def attend(l, b):
                def body(n, kind):
                    for s in range(STEPS[l]):
                        split_prob(step_no(l, b, n, s), s % 2, kind != "first" or s >= 2)
                    for jobs in body_jobs(l, b, n, kind):
                        for a, bank, name, ct in jobs:
                            if name == "Z":
                                add_x(b, n, a, bank, ct)
                attend_loop(pool, l, body)
                for a, bank, name, ct in after_last(l, b):
                    if name == "Z":
                        add_x(b, NCH, a, bank, ct)

            with pool.Fori(0, B) as b:
                for l in range(2):
                    with pool.Fori(0, NCH // 2) as cc:
                        for par in range(2):
                            split_x(l, b, cc * 2 + par, par)
                    attend(l, b)

        @block.scalar
        def _(act):
            act.dma_start(w_sb, w_v).then_inc(w_in, 16)
            act.dma_start(wo[:, :], wo_d).then_inc(cols_in, 16)
            act.dma_start(cols[:, :], cols_d).then_inc(cols_in, 16)
            act.wait_ge(cols_in, 32)
            for ct, first_credit in enumerate((o_act, psums_ready)):
                nc.scalar.activation(gbv[:, ct:ct + 1], cols[:, COL_BV + ct:COL_BV + ct + 1], ACT.Copy,
                                     scale=cols[:, COL_G0:COL_G0 + 1]).then_inc(first_credit, ONE)

            def round_x(l, b, c, par):
                if l == 0:
                    act.wait_ge(x_in[par], b * (16 * NCH // 2) + (c - par) * 8 + 16)
                else:
                    act.wait_ge(x1_ready, ONE + b * NCH + c + 1)
                act.wait_ge(pj_full, CREDIT - 4 + 4 * chunk_no(l, b, c))
                nc.scalar.activation(xh[par][:, :, :], x_sb[:, :, chunk(c)], ACT.Copy).then_inc(xh_ready, 1)

            def copy_q_ahead(n):
                nc.scalar.activation(q_ahead[:, :], queries[0:R3, chunk(n)].bitcast(f32),
                                     ACT.Copy).then_inc(q_ahead_ready, 1)

            def high(l, b, c):
                pc = chunk_no(l, b, c)

                def full(k):
                    act.wait_ge(pj_full, CREDIT + 4 * pc + (k + 1))

                def biased(dst, src, col):
                    nc.scalar.activation(dst, src, ACT.Identity, bias=cols[0:R3, col:col + 1]).then_inc(hi_ready, 1)

                if l == 0:
                    full(0)
                    biased(keys[0:R3, chunk(c)], pj[0][0:R3, :], COL_BQ)
                    full(1)
                    biased(queries[0:R3, chunk(c)], pj[1][0:R3, :], COL_BK)
                    for k in (2, 3):
                        full(k)
                        nc.scalar.activation(vh[:, ds(c * SUBS + 2 * (k - 2), 2), :],
                                             pj[k].rearrange("p (t m) -> p t m", t=2), ACT.Copy).then_inc(hi_ready, 1)
                else:
                    act.wait_ge(pj_drained, CREDIT + 4 * pc + 2)
                    biased(keys[0:R3, ds(c * P, P)], ppool[:, :], COL_BPHI)
                    full(2)
                    biased(queries[0:R3, chunk(c)], pj[1][0:R3, :], COL_BTH)
                    full(3)
                    nc.scalar.activation(vh_flat[:, ds(c * DV, DV)], pj[3][:, 0:P], ACT.Copy).then_inc(hi_ready, 1)

            def exps(g, i, wait_buffers):
                act.wait_ge(s_full, g + 1)
                if wait_buffers:
                    act.wait_ge(pl_ready, g - 1)
                    act.wait_ge(acc_done, 2 * g - 2)
                nc.scalar.activation(prob[i], s_ps[i][:, :, :], ACT.Exp).then_inc(p_ready, 1)
                if wait_buffers:
                    act.wait_ge(av_h, g - 1)
                nc.scalar.activation(prob_h[i][:, :, :], s_ps[i][:, :, :], ACT.Exp).then_inc(ph_ready, 1)

            def copy_o(l, b, n):
                act.wait_ge(av_l, step_no(l, b, n, 0))
                if l == 0:
                    act.wait_ge(x1_ready, ONE + b * NCH + n - 1)
                else:
                    act.wait_ge(norm_done, ONE + chunk_no(l, b, n - 1))
                nc.scalar.activation(osb[:, 0, :], o_ps[0][:, :], ACT.Copy).then_inc(o_act, 1)

            def copy_acc(l, b, n):
                act.wait_ge(acc_done, 2 * step_no(l, b, n, 0))
                nc.scalar.activation(psums[:, :], acc[:, :], ACT.Copy).then_inc(psums_ready, 1)

            def make_rdiag(l, b, n, a, bank):
                act.wait_ge(aux_free[bank], ONE + a + 1)
                for s in range(SUBS):
                    last = nc.scalar.activation(rdiag[:, s * P:(s + 1) * P], ident[:, :], ACT.Copy,
                                                scale=rsum[:, s:s + 1])
                last.then_inc(rdiag_ready, 1)

            def drain(l, b, n, a, bank, name, ct):
                if name == "D2":
                    act.wait_ge(norm_done, ONE + chunk_no(l, b, n - 1))
                    act.wait_ge(aux_full[bank], a + 1)
                    nc.scalar.activation(rb[:, :], aux_bank[bank][:, :], ACT.Copy).then_inc(aux_free[bank], 1)
                elif name == "Z":
                    act.wait_ge(y_ready, (b * NCH + n - 1) * CT + (ct + ONE))
                    act.wait_ge(aux_full[bank], a + 1)
                    nc.scalar.activation(zc[:, :], aux_bank[bank][:, :], ACT.Identity, bias=cb[:, ct:ct + 1],
                                         scale=cols[:, COL_G1:COL_G1 + 1]).then_inc(aux_free[bank], 1)

            def attend(l, b):
                def body(n, kind):
                    jobs = body_jobs(l, b, n, kind)
                    d1 = [j for step in jobs for j in step if j[2] == "D1"]
                    for s in range(STEPS[l]):
                        exps(step_no(l, b, n, s), s % 2, kind != "first" or s >= 2)
                        if s == 0:
                            if kind != "first":
                                copy_acc(l, b, n)
                            if kind != "last":
                                for k in range(l + 1):
                                    act.wait_ge(aux_full[k], aux_base(l, b, n, k) - MS[k])
                                copy_q_ahead(n + DIST[l])
                            if kind != "first":
                                copy_o(l, b, n)
                        if s == 1 and kind != "first":
                            make_rdiag(l, b, n, *d1[0][:2])
                        for a, bank, name, arg in jobs[s]:
                            if name in ("D2", "Z"):
                                drain(l, b, n, a, bank, name, arg)
                attend_loop(act, l, body)
                copy_acc(l, b, NCH)
                copy_o(l, b, NCH)
                for a, bank, name, arg in after_last(l, b):
                    if name == "D1":
                        make_rdiag(l, b, NCH, a, bank)
                    else:
                        drain(l, b, NCH, a, bank, name, arg)

            def project(l, b):
                def pair(cc, last):
                    for par in range(2):
                        if not (last and par == 1):
                            round_x(l, b, cc * 2 + (par + 1), 1 - par)
                        high(l, b, cc * 2 + par)
                        if l == 0 and isinstance(cc, int) and cc == 0 and par == 0:
                            act.wait_ge(pj_drained, CREDIT + 4 * chunk_no(0, b, 0) + 2)
                            copy_q_ahead(0)
                round_x(l, b, 0, 0)
                pair(0, False)
                with act.Fori(1, NCH // 2 - 1) as cc:
                    pair(cc, False)
                pair(NCH // 2 - 1, True)

            act.wait_ge(pj_drained, CREDIT)
            with act.Fori(0, B) as b:
                project(0, b)
                attend(0, b)
                project(1, b)
                for n in range(DIST[1]):
                    if n == 0:
                        act.wait_ge(pj_drained, CREDIT + 4 * chunk_no(1, b, NCH))
                    else:
                        for k in range(2):
                            act.wait_ge(aux_full[k], aux_start(1, b, k) + n * STS[1][k])
                    copy_q_ahead(n)
                attend(1, b)

        @block.vector
        def _(dve):
            for k, first_credit in enumerate((aux_free[0], aux_free[1], norm_done, x1_ready)):
                nc.vector.memset(keys[R3:P, ds(k * N // 4, N // 4)].bitcast(f32), 1.0).then_inc(first_credit, ONE)
            dve.wait_ge(w_in, 16)
            nc.vector.tensor_copy(wh[:, :, :], w_sb).then_inc(dve_setup, 1)
            dve.wait_ge(dve_setup, 1)
            nc.vector.tensor_tensor(out=wl[:, :, :], in0=w_sb, in1=wh[:, :, :].bitcast(f32),
                                    op=ALU.subtract).then_inc(w_ready, 1)
            dve.wait_ge(cols_in, 32)
            dve.wait_ge(consts_ready, 1)
            nc.vector.tensor_copy(ident_r[:, :], ident[:, :]).then_inc(o_dve, ONE)
            dve.wait_ge(pj_full, CREDIT)
            nc.vector.tensor_tensor(out=cb[:, :], in0=cols[:, COL_BO:COL_BO + CT], in1=aux[:, 0:CT],
                                    op=ALU.add).then_inc(dve_setup, 1)
            dve.wait_ge(dve_setup, 2)
            nc.vector.tensor_scalar(cb[:, :], cb[:, :], cols[:, COL_G1:COL_G1 + 1], None,
                                    ALU.mult).then_inc(pj_drained, CREDIT)

            def st_drain(a, bank, sub, c):
                dve.wait_ge(aux_full[bank], a + 1)
                nc.vector.tensor_reduce(out=mx[:, sub, c], in_=aux_bank[bank][:, :], axis=AX.X,
                                        op=ALU.max).then_inc(aux_free[bank], 1)

            def finish_max(l, a, bank, target):
                dve.wait_ge(aux_free[bank], ONE + a + 1)
                nc.vector.tensor_reduce(out=nm[:, :], in_=mx[:, :, 0:KEYS[l] // CH], axis=AX.X, op=ALU.max,
                                        negate=True).then_inc(mx_chain, 1)
                dve.wait_ge(mx_chain, 2 * target + 1)
                nc.vector.tensor_copy(nm_wide[:, :, R3], nm[:, :]).then_inc(mx_chain, 1)
                dve.wait_ge(mx_chain, 2 * target + 2)
                nc.vector.tensor_tensor(out=nm_wide[:, :, R3 + 1], in0=nm[:, :], in1=nm_wide[:, :, R3].bitcast(f32),
                                        op=ALU.subtract).then_inc(nm_ready, 1)

            def m_drain(a, n):
                dve.wait_ge(aux_full[0], a + 1)
                nc.vector.tensor_copy(queries[R3:P, chunk(n)], aux[R3:P, :]).then_inc(aux_free[0], 1)

            def low(dst, src, scalar, hi):
                if scalar is None:
                    return nc.vector.tensor_tensor(out=dst, in0=src, in1=hi.bitcast(f32), op=ALU.subtract)
                return nc.vector.scalar_tensor_tensor(out=dst, in0=src, scalar=scalar, in1=hi.bitcast(f32),
                                                      op0=ALU.add, op1=ALU.subtract)

            LK = slice(2 * DK, R3)
            LQ = slice(DK, 2 * DK)

            def project0(b, c, st):
                pc = chunk_no(0, b, c)
                a = b * AUX_BATCH[0] + (c - 1) * SUBS
                for k in range(4):
                    dve.wait_ge(hi_ready, hi_no(0, b, c, k) + 1)
                    if k == 0:
                        ins = low(keys[LK, chunk(c)], pj[0][LK, :], cols[LK, COL_BQ:COL_BQ + 1], keys[LK, chunk(c)])
                    elif k == 1:
                        ins = low(queries[LQ, chunk(c)], pj[1][LQ, :], cols[LQ, COL_BK:COL_BK + 1],
                                  queries[LQ, chunk(c)])
                    else:
                        tiles = ds(c * SUBS + 2 * (k - 2), 2)
                        ins = low(vl[:, tiles, :], pj[k].rearrange("p (t m) -> p t m", t=2), None, vh[:, tiles, :])
                    ins.then_inc(pj_drained, 1)
                    if st:
                        st_drain(a + k, 0, k, ds(c - 1, 1))

            def pool_max(dst, src):
                return nc.vector.tensor_reduce(
                    out=dst.rearrange("p (h w) -> p h w", w=PW),
                    in_=src.rearrange("p (h a w b) -> p h w a b", a=2, b=2, w=PW), axis=AX.XY, op=ALU.max)

            def project1(b, c):
                pc = chunk_no(1, b, c)
                dve.wait_ge(pj_drained, CREDIT + 4 * pc)
                dve.wait_ge(pj_full, CREDIT + 4 * pc + 1)
                pool_max(gpool[:, :], pj[2]).then_inc(pj_drained, 1)
                dve.wait_ge(pj_full, CREDIT + 4 * pc + 2)
                pool_max(ppool[:, :], pj[0][0:R3, :]).then_inc(pj_drained, 1)
                dve.wait_ge(hi_ready, hi_no(1, b, c, 0) + 1)
                low(keys[LK, ds(c * P, P)], ppool[LK, :], cols[LK, COL_BPHI:COL_BPHI + 1], keys[LK, ds(c * P, P)])
                dve.wait_ge(hi_ready, hi_no(1, b, c, 1) + 1)
                low(queries[LQ, chunk(c)], pj[1][LQ, :], cols[LQ, COL_BTH:COL_BTH + 1],
                    queries[LQ, chunk(c)]).then_inc(pj_drained, 1)
                dve.wait_ge(hi_ready, hi_no(1, b, c, 2) + 1)
                low(vl_flat[:, ds(c * DV, DV)], pj[3][:, 0:P], None,
                    vh_flat[:, ds(c * DV, DV)]).then_inc(pj_drained, 1)

            def add_prob(l, b, n, s, t):
                g, i = step_no(l, b, n, s), s % 2
                if t == 0:
                    dve.wait_ge(p_ready, g + 1)
                if s == 0 and t == 0:
                    dve.wait_ge(psums_ready, ONE + chunk_no(l, b, n))
                    nc.vector.tensor_copy(acc[:, :], prob[i][:, 0, :]).then_inc(acc_done, 1)
                else:
                    dve.wait_ge(acc_done, 2 * g + t)
                    nc.vector.tensor_tensor(out=acc[:, :], in0=prob[i][:, t, :], in1=acc[:, :],
                                            op=ALU.add).then_inc(acc_done, 1)

            def drain(l, b, n, a, bank, name, arg):
                if name == "ST":
                    st_drain(a, bank, arg % SUBS, slice(arg // SUBS, arg // SUBS + 1))
                elif name == "M":
                    m_drain(a, n + DIST[l])
                elif name == "D1":
                    dve.wait_ge(aux_full[bank], a + 1)
                    nc.vector.reciprocal(rsum[:, :], aux_bank[bank][:, 0:SUBS]).then_inc(aux_free[bank], 1)

            def normalise(l, b, n, k):
                if l == 1:
                    nc.vector.tensor_tensor(out=osb[:, 1, :], in0=osb[:, 0, :], in1=rb[:, :],
                                            op=ALU.mult).then_inc(norm_done, 1)
                elif k < CT:
                    ins = nc.vector.scalar_tensor_tensor(out=osb[:, k, :], in0=osb[:, k, :],
                                                         scalar=cols[:, COL_G0:COL_G0 + 1], in1=rb[:, :],
                                                         op0=ALU.mult, op1=ALU.mult)
                    if k == CT - 1:
                        ins.then_inc(norm_done, 1)
                else:
                    ct = k - CT
                    dve.wait_ge(norm_done, ONE + chunk_no(0, b, n))
                    ins = nc.vector.scalar_tensor_tensor(
                        out=x_sb[:, ct, chunk(n - 1)], in0=osb[:, ct, :], scalar=gbv[:, ct:ct + 1],
                        in1=x_sb[:, ct, chunk(n - 1)], op0=ALU.add, op1=ALU.add)
                    if ct == CT - 1:
                        ins.then_inc(x1_ready, 1)

            def before_normalise(l, b, n, d2):
                dve.wait_ge(aux_free[d2[1]], ONE + d2[0] + 1)
                dve.wait_ge(o_act, ONE + chunk_no(l, b, n))

            def copy_o(b, n):
                dve.wait_ge(av_l, step_no(0, b, n, 0))
                dve.wait_ge(x1_ready, ONE + b * NCH + n - 1)
                nc.vector.tensor_copy(osb[:, 1, :], o_ps[1][:, :]).then_inc(o_dve, 1)

            def attend(l, b):
                def body(n, kind):
                    jobs = body_jobs(l, b, n, kind)
                    d2 = [j for step in jobs for j in step if j[2] == "D2"]
                    if l == 0 and kind != "first":
                        copy_o(b, n)
                    for s in range(STEPS[l]):
                        mine = [j for j in jobs[s] if j[2] in ("ST", "M", "D1")]
                        for k in range(max(len(mine), 3)):
                            if k < len(mine):
                                drain(l, b, n, *mine[k])
                                if mine[k][2:] == ("ST", NST[l] - 1):
                                    finish_max(l, *mine[k][:2], chunk_no(l, b, n + DIST[l]))
                            if k < 2:
                                add_prob(l, b, n, s, k)
                        if kind != "first" and s in NORM_STEPS[l]:
                            k = NORM_STEPS[l].index(s)
                            if k == 0:
                                before_normalise(l, b, n, d2[0])
                            normalise(l, b, n, k)
                attend_loop(dve, l, body)
                if l == 0:
                    copy_o(b, NCH)
                jobs = after_last(l, b)
                drain(l, b, NCH, *jobs[0])
                before_normalise(l, b, NCH, jobs[1])
                for k in range(len(NORM_STEPS[l])):
                    normalise(l, b, NCH, k)

            with dve.Fori(0, B) as b:
                project0(b, 0, False)
                with dve.Fori(1, NCH) as c:
                    project0(b, c, True)
                jobs = prologue_jobs(0, b, 0)
                for a, bank, name, arg in jobs[-1 - SUBS:-1]:
                    st_drain(a, bank, arg % SUBS, slice(NCH - 1, NCH))
                finish_max(0, *jobs[-2][:2], chunk_no(0, b, 0))
                m_drain(jobs[-1][0], 0)
                attend(0, b)
                with dve.Fori(0, NCH) as c:
                    project1(b, c)
                for n in range(DIST[1]):
                    jobs = prologue_jobs(1, b, n)
                    for a, bank, name, arg in jobs[:-1]:
                        st_drain(a, bank, arg % SUBS, slice(arg // SUBS, arg // SUBS + 1))
                    finish_max(1, *jobs[-2][:2], chunk_no(1, b, n))
                    m_drain(jobs[-1][0], n)
                attend(1, b)

        @block.tensor
        def _(pe):
            mm = nc.tensor.matmul
            pe.wait_ge(cols_in, 32)
            for ct in range(CT):
                last = mm(aux[:, ct:ct + 1], wo[:, ct * P:(ct + 1) * P], cols[:, COL_BG:COL_BG + 1],
                          start=True, stop=True)
            last.then_inc(pj_full, CREDIT)
            pe.wait_ge(w_ready, 1)
            pe.wait_ge(pj_drained, CREDIT)

            def st_job(a, bank, sub, c):
                pe.wait_ge(aux_free[bank], ONE + a)
                mm(aux_bank[bank][:, :], q_ahead[:, sub * P:(sub + 1) * P], keys[0:R3, chunk(c)],
                   start=True, stop=True).then_inc(aux_full[bank], 1)

            def m_job(a, target):
                pe.wait_ge(aux_free[0], ONE + a)
                pe.wait_ge(nm_ready, target + 1)
                for s in range(SUBS):
                    last = mm(aux[:, s * P:(s + 1) * P], nm_wide[:, s, :], ident_r[:, :], start=True, stop=True)
                last.then_inc(aux_full[0], 1)

            def conv(dst, w0, width, par, wait):
                first = True
                for kt in range(CT):
                    for w in (wh, wl):
                        mm(dst, w[:, kt, w0:w0 + width], xh[par][:, kt, :], start=first, stop=False)
                        first = False
                if wait is not None:
                    pe.wait_ge(xl_ready, wait)
                for kt in range(CT):
                    last = mm(dst, wh[:, kt, w0:w0 + width], xl[par][:, kt, :], start=False, stop=kt == CT - 1)
                return last

            def project0(b, c, par, st):
                pc = chunk_no(0, b, c)
                a = b * AUX_BATCH[0] + (c - 1) * SUBS
                for k in range(4):
                    pe.wait_ge(pj_drained, CREDIT - 4 + 4 * pc + (k + 1))
                    if k == 0:
                        pe.wait_ge(xh_ready, pc + 1)
                        last = conv(pj[0][0:R3, :], W_Q, R3, par, pc + 1)
                    elif k == 1:
                        last = conv(pj[1][0:R3, :], W_K, R3, par, None)
                    else:
                        for t in range(2):
                            pos = slice((2 * (k - 2) + t) * P, (2 * (k - 2) + t + 1) * P)
                            dst = pj[k][:, t * C:(t + 1) * C]
                            first = True
                            for kt in range(CT):
                                for w in (wh, wl):
                                    mm(dst, xh[par][:, kt, pos], w[:, kt, W_V:W_V + C], start=first, stop=False)
                                    first = False
                            for kt in range(CT):
                                last = mm(dst, xl[par][:, kt, pos], wh[:, kt, W_V:W_V + C], start=False,
                                          stop=kt == CT - 1)
                    last.then_inc(pj_full, 1)
                    if st:
                        if k == 0:
                            pe.wait_ge(q_ahead_ready, chunk_no(0, b, 0) + 1)
                        st_job(a + k, 0, k, c - 1)

            def project1(b, c, par):
                pc = chunk_no(1, b, c)
                for k, (bank, w0, width) in enumerate(((2, W_G, DV), (0, W_PHI, R3), (1, W_TH, R3))):
                    pe.wait_ge(pj_drained, CREDIT - 4 + 4 * pc + (k + 1))
                    if k == 0:
                        pe.wait_ge(xh_ready, pc + 1)
                    conv(pj[bank][0:width, :], w0, width, par, pc + 1 if k == 0 else None).then_inc(pj_full, 1)
                pe.wait_ge(pj_drained, CREDIT + 4 * pc)
                pe.wait_ge(pj_drained, CREDIT + 4 * pc + 1)
                nc.tensor.transpose(pj[3][:, 0:P], gpool[:, :], ident[:, :]).then_inc(pj_full, 1)

            def scores(l, n, s):
                i = s % 2
                for t in range(2):
                    kt = 2 * s + t
                    last = mm(s_ps[i][:, t, :], keys[:, kt * P:(kt + 1) * P], queries[:, chunk(n)],
                              start=True, stop=True)
                last.then_inc(s_full, 1)

            def av(l, s, low, tile=None):
                i = s % 2
                for t in range(2) if tile is None else (tile,):
                    kt = 2 * s + t
                    for ct in range(VT[l]):
                        at = (kt * VT[l] + ct) * P
                        v_h, v_l = vh_flat[:, at:at + P], vl_flat[:, at:at + P]
                        if low:
                            last = mm(o_ps[ct][:, :], v_h, prob_l[i][:, t, :], start=False, stop=kt == KT[l] - 1)
                        else:
                            mm(o_ps[ct][:, :], v_h, prob_h[i][:, t, :], start=kt == 0, stop=False)
                            last = mm(o_ps[ct][:, :], v_l, prob_h[i][:, t, :], start=False, stop=False)
                if tile != 0:
                    last.then_inc(av_l if low else av_h, 1)

            def job(l, b, n, a, bank, name, arg):
                dst = aux_bank[bank]
                if name == "ST":
                    if arg == 0:
                        pe.wait_ge(q_ahead_ready, chunk_no(l, b, n + DIST[l]) + 1)
                    st_job(a, bank, arg % SUBS, arg // SUBS)
                    return
                if name == "M":
                    m_job(a, chunk_no(l, b, n + DIST[l]))
                    return
                pe.wait_ge(aux_free[bank], ONE + a)
                if name == "D1":
                    pe.wait_ge(psums_ready, ONE + chunk_no(l, b, n))
                    for s in range(SUBS):
                        last = mm(dst[:, s:s + 1], psums[:, s * P:(s + 1) * P], ones[:, 0:1], start=True, stop=True)
                elif name == "D2":
                    pe.wait_ge(rdiag_ready, chunk_no(l, b, n))
                    last = mm(dst[:, :], ones[:, :], rdiag[:, :], start=True, stop=True)
                else:
                    pe.wait_ge(norm_done, ONE + chunk_no(l, b, n))
                    last = mm(dst[:, :], wo[:, arg * P:(arg + 1) * P], osb[:, 1, :], start=True, stop=True)
                last.then_inc(aux_full[bank], 1)

            SLOTS = {0: (), 1: (1,), 2: (0, 2), 3: (0, 1, 2), 4: (0, 1, 2, 3)}

            def attend(l, b):
                def body(n, kind):
                    jobs = body_jobs(l, b, n, kind)
                    for s in range(STEPS[l]):
                        g = step_no(l, b, n, s)

                        def slot(k):
                            for at, j in zip(SLOTS[len(jobs[s])], jobs[s]):
                                if at == k:
                                    job(l, b, n, *j)

                        if s + 1 < STEPS[l]:
                            scores(l, n, s + 1)
                        elif not (isinstance(n, int) and n == NCH - 1):
                            pe.wait_ge(aux_free[0], ONE + (aux_base(l, b, n + 1) if l == 0 else aux_base(l, b, n)))
                            scores(l, n + 1, 0)
                        slot(0)
                        if s:
                            pe.wait_ge(pl_ready, g)
                            av(l, s - 1, True)
                        slot(1)
                        if s == 0:
                            pe.wait_ge(o_act, ONE + chunk_no(l, b, n))
                            if l == 0:
                                pe.wait_ge(o_dve, ONE + b * NCH + n)
                        pe.wait_ge(ph_ready, g + 1)
                        av(l, s, False, 0)
                        slot(2)
                        av(l, s, False, 1)
                        slot(3)
                    pe.wait_ge(pl_ready, step_no(l, b, n, STEPS[l]))
                    av(l, STEPS[l] - 1, True)

                pe.wait_ge(pj_drained, CREDIT + 4 * chunk_no(l, b, NCH))
                pe.wait_ge(aux_free[0], ONE + aux_base(l, b, 0))
                if l == 0:
                    pe.wait_ge(aux_free[1], ONE + aux_start(0, b, 1))
                scores(l, 0, 0)
                attend_loop(pe, l, body)
                for j in after_last(l, b):
                    job(l, b, NCH, *j)

            with pe.Fori(0, B) as b:
                project0(b, 0, 0, False)
                project0(b, 1, 1, True)
                with pe.Fori(1, NCH // 2) as cc:
                    for par in range(2):
                        project0(b, cc * 2 + par, par, True)
                pe.wait_ge(pj_drained, CREDIT + 4 * chunk_no(0, b, NCH))
                jobs = prologue_jobs(0, b, 0)
                for a, bank, name, arg in jobs[-1 - SUBS:-1]:
                    st_job(a, bank, arg % SUBS, NCH - 1)
                m_job(jobs[-1][0], chunk_no(0, b, 0))
                attend(0, b)
                with pe.Fori(0, NCH // 2) as cc:
                    for par in range(2):
                        project1(b, cc * 2 + par, par)
                pe.wait_ge(o_dve, ONE + b * NCH + NCH)
                for n in range(DIST[1]):
                    pe.wait_ge(q_ahead_ready, chunk_no(1, b, n) + 1)
                    jobs = prologue_jobs(1, b, n)
                    for a, bank, name, arg in jobs[:-1]:
                        st_job(a, bank, arg % SUBS, arg // SUBS)
                    m_job(jobs[-1][0], chunk_no(1, b, n))
                attend(1, b)


def kernel(x, L0_conv_Wq, L0_conv_bq, L0_conv_Wk, L0_conv_bk, L0_conv_Wv, L0_conv_bv, L0_conv_gamma,
           L1_conv_theta_w, L1_conv_theta_b, L1_conv_phi_w, L1_conv_phi_b, L1_conv_g_w, L1_conv_g_b,
           L1_conv_out_w, L1_conv_out_b, L1_conv_gamma):
    import numpy as np
    import concourse.bacc as bacc
    from concourse.bass_utils import run_bass_kernel_spmd

    def thrice(w):
        return np.concatenate([np.asarray(w).T] * 3, axis=1)

    w = np.concatenate([thrice(L0_conv_Wq), thrice(L0_conv_Wk), np.asarray(L0_conv_Wv).T, thrice(L1_conv_phi_w),
                        thrice(L1_conv_theta_w), np.asarray(L1_conv_g_w).T], axis=1)
    cols = np.zeros((P, NCOLS), np.float32)
    for col, v in ((COL_BQ, L0_conv_bq), (COL_BK, L0_conv_bk), (COL_BPHI, L1_conv_phi_b), (COL_BTH, L1_conv_theta_b)):
        cols[:R3, col] = np.concatenate([np.asarray(v)] * 3)
    cols[:, COL_BV:COL_BV + CT] = np.asarray(L0_conv_bv).reshape(CT, P).T
    cols[:, COL_BG] = np.asarray(L1_conv_g_b)
    cols[:, COL_BO:COL_BO + CT] = np.asarray(L1_conv_out_b).reshape(CT, P).T
    cols[:, COL_G0] = np.broadcast_to(np.asarray(L0_conv_gamma), (P,))
    cols[:, COL_G1] = np.broadcast_to(np.asarray(L1_conv_gamma), (P,))
    arrays = {
        "x": np.ascontiguousarray(np.asarray(x).reshape(B, C, N)),
        "w_in": np.ascontiguousarray(w),
        "w_out": np.ascontiguousarray(np.asarray(L1_conv_out_w).T),
        "columns": cols,
    }
    f32 = mybir.dt.float32
    nc = bacc.Bacc("TRN2", target_bir_lowering=False, num_devices=1)
    ins = [nc.dram_tensor(k, a.shape, f32, kind="ExternalInput").ap() for k, a in arrays.items()]
    y = nc.dram_tensor("y", (B, C, N), f32, kind="ExternalOutput").ap()
    build(nc, *ins, y)
    r = run_bass_kernel_spmd(nc, [arrays], core_ids=[0])
    return r.results[0]["y"].reshape(B, C, IMG_W, IMG_W)
```

```python
from contextlib import ExitStack

import concourse.bass as bass
from concourse import mybir

B, C, N = 4, 256, 4096
P = 128
DK = C // 8
DV = C // 2
CT = C // P
R3 = 3 * DK
CH = 512
NCH = N // CH
SUBS = CH // P
IMG_W = 64
PW = IMG_W // 2
CHROWS = CH // IMG_W
KEYS = (N, N // 4)
KT = tuple(k // P for k in KEYS)
STEPS = tuple(t // 2 for t in KT)
DIST = (1, 2)
VT = (CT, 1)
NST = tuple(SUBS * k // CH for k in KEYS)
PRO_STS = tuple((n // 2, n // 2) for n in NST)
STS = ((NST[0], 0), (NST[1] // 2, NST[1] // 2))
MS = (1, 0)
EPS = ((2, 0), (2, 2))
WCOLS = 2 * R3 + C + DV
W_KQ, W_V, W_G = (0, R3), 2 * R3, 2 * R3 + C
COL_KQ, COL_BV, COL_BG, COL_BO, COL_G0, COL_G1 = (0, 1), 2, 4, 5, 7, 8
NCOLS = 9

STEP_BATCH = NCH * sum(STEPS)
CHUNK_BATCH = 2 * NCH
AUX_LAYER = tuple(tuple(DIST[l] * (PRO_STS[l][k] + MS[k]) + (NCH - DIST[l]) * (STS[l][k] + MS[k])
                        + NCH * EPS[l][k] for k in range(2)) for l in range(2))
AUX_BATCH = tuple(AUX_LAYER[0][k] + AUX_LAYER[1][k] for k in range(2))
HI_CHUNK = (5, 4)
FILLS = 3
DRAINS = 4
HI_BATCH = NCH * sum(HI_CHUNK)
CREDIT = 8
ONE = 1


def step_no(l, b, n, s):
    return b * STEP_BATCH + (l * NCH * STEPS[0] + s) + n * STEPS[l]


def chunk_no(l, b, n):
    return b * CHUNK_BATCH + n + l * NCH


def aux_base(l, b, n, k=0):
    off = l * AUX_LAYER[0][k] + DIST[l] * (PRO_STS[l][k] + MS[k])
    if isinstance(n, int) and n == 0:
        return b * AUX_BATCH[k] + off
    off += STS[l][k] + MS[k]
    full = NCH - 1 - DIST[l]
    each = STS[l][k] + MS[k] + EPS[l][k]
    if isinstance(n, int) and n > full + 1:
        return b * AUX_BATCH[k] + (off + full * each + (n - 1 - full) * EPS[l][k])
    return b * AUX_BATCH[k] + off + (n - 1) * each


def aux_start(l, b, k=0):
    return b * AUX_BATCH[k] + l * AUX_LAYER[0][k]


def aux_maxima(b, c, sub):
    return b * AUX_BATCH[sub % 2] + (c * (SUBS // 2) + sub // 2)


def bank_of(l, name, arg):
    return {"ST": arg % 2, "M": 0, "D1": 1, "D2": 0, "Z": arg}[name] if l else 0


def hi_no(l, b, c, k):
    return b * HI_BATCH + (l * NCH * HI_CHUNK[0] + k) + c * HI_CHUNK[l]


ST_STEPS = (0, 2, 0, 2, 3, 2, 3, 2, 2, 3, 2, 2, 3, 2, 0, 0)
PLACES = {0: (), 2: (1, 8), 3: (0, 5, 10)}
PLANS = (
    [[["ST", 0, place] for place in PLACES[st]] for st in ST_STEPS],
    [[["ST", 0, 0], ["D1", 0, 4], ["ST", 1, 6]],
     [["ST", 2, 0], ["ST", 3, 2], ["D2", 0, 4]],
     [["ST", 4, 1], ["ST", 5, 2], ["ST", 6, 4], ["ST", 7, 5]],
     [["Z", 0, 2], ["Z", 1, 6], ["M", 0, 6]]])
PLANS[0][0] = [["ST", 0, 0], ["ST", 0, 7], ["D1", 0, 12]]
PLANS[0][2] = [["D2", 0, 0], ["ST", 0, 10]]
PLANS[0][14] = [["ST", 0, 0], ["M", 0, 8]]
for _number, _job in enumerate([_job for _jobs in PLANS[0] for _job in _jobs if _job[0] == "ST"]):
    _job[1] = _number
NORM_STEPS = ((4, 5, 6, 7), (2,))
NORM_AT = 2


def schedule(l, kind):
    left_out = {"first": ("D1", "D2", "Z"), "mid": (), "last": ("ST", "M")}[kind]
    assert sum(j[0] == "ST" for jobs in PLANS[l] for j in jobs) == NST[l]
    return [[j for j in jobs if j[0] not in left_out] for jobs in PLANS[l]]


def behind_maxima(l, n, k):
    kind = "first" if isinstance(n, int) and n <= 1 else "mid"
    names = [j[0] for jobs in schedule(l, kind) for j in jobs if bank_of(l, *j[:2]) == k]
    return names[::-1].index("ST")


def tail_jobs(l):
    return [("D1", 0), ("D2", 0), ("Z", 0), ("Z", 1)][:4 if l else 2]


def build(nc, x_d, w_d, wo_d, cols_d, y_d):
    f32, f32r = mybir.dt.float32, mybir.dt.float32r
    ALU, ACT, AX = mybir.AluOpType, mybir.ActivationFunctionType, mybir.AxisListType
    ds = bass.ds

    x_v = x_d.rearrange("b (t p) n -> p (b t) n", p=P)
    y_v = y_d.rearrange("b (t p) n -> p (b t) n", p=P)
    w_v = w_d.rearrange("(t p) m -> p t m", p=P)

    ctx = ExitStack()
    with ctx:
        def sb(name, shape, dt=f32):
            return ctx.enter_context(nc.sbuf_tensor(name, shape, dt))

        def pb(name, shape):
            return ctx.enter_context(nc.psum_tensor(name, shape, f32))

        def sem(name):
            return ctx.enter_context(nc.semaphore(name))

        x_sb = sb("x_sb", [P, CT, N])
        keys = sb("keys", [P, N], f32r)
        queries = sb("queries", [P, N], f32r)
        q_ahead = sb("q_ahead", [R3, CH], f32r)
        vh = sb("vh", [P, KT[0], C], f32r)
        vl = sb("vl", [P, KT[0], C], f32r)
        vh_flat = vh[:, :, :].rearrange("p t m -> p (t m)")
        vl_flat = vl[:, :, :].rearrange("p t m -> p (t m)")
        prob_sb = sb("prob", [P, 2, 2, CH])
        prob = [prob_sb[:, i, :, :] for i in range(2)]
        prob_h = [sb(f"prob_h{i}", [P, 2, CH], f32r) for i in range(2)]
        prob_l = [sb(f"prob_l{i}", [P, 2, CH], f32r) for i in range(2)]
        xh = [sb(f"xh{i}", [P, CT, CH], f32r) for i in range(2)]
        xl = [sb(f"xl{i}", [P, CT, CH], f32r) for i in range(2)]
        w_sb = prob_sb[:, :, :, :].rearrange("p i t c -> p (i t c)")[:, 0:CT * WCOLS].rearrange(
            "p (t m) -> p t m", t=CT)
        wh = sb("wh", [P, CT, WCOLS], f32r)
        wl = sb("wl", [P, CT, WCOLS], f32r)
        wo = sb("wo", [DV, C])
        cols = sb("cols", [P, NCOLS])
        gbv = sb("gbv", [P, CT])
        cb = sb("cb", [P, CT])
        ident = sb("ident", [P, P])
        ident_r = sb("ident_r", [P, P], f32r)
        ones = sb("ones", [P, P])
        mx = sb("mx", [P, SUBS, NCH])
        nm = sb("nm", [P, SUBS])
        nm_wide = sb("nm_wide", [P, SUBS, P], f32r)
        psums = sb("psums", [P, CH])
        rsum = sb("rsum", [P, SUBS])
        rb = sb("rb", [P, CH])
        osb = sb("osb", [P, CT, CH])
        zc = sb("zc", [P, CT, CH])
        gpool = sb("gpool", [P, P])
        ppool = sb("ppool", [2 * DK, P])

        s_ps = [pb(f"s_ps{i}", [P, 2, CH]) for i in range(2)]
        o_ps = [pb(f"o_ps{i}", [P, CH]) for i in range(2)]
        aux = pb("aux", [P, CH])
        aux_bank = (aux, o_ps[1])
        acc = pb("acc", [P, CH])
        pj_kq = (s_ps[0][:, 0, :], s_ps[0][:, 1, :])
        pj_v = (s_ps[1][:, 0, :], s_ps[1][:, 1, :])

        w_in, cols_in = sem("w_in"), sem("cols_in")
        x_in = [sem("x_in0"), sem("x_in1")]
        y_out = [sem("y_out0"), sem("y_out1")]
        ident_ready, consts_ready, w_ready, dve_setup = (
            sem("ident_ready"), sem("consts_ready"), sem("w_ready"), sem("dve_setup"))
        xh_ready = sem("xh_ready")
        xl_ready = sem("xl_ready")
        pj_full = sem("pj_full")
        pj_drained = sem("pj_drained")
        hi_ready = sem("hi_ready")
        q_ahead_ready = sem("q_ahead_ready")
        s_full = sem("s_full")
        p_ready = sem("p_ready")
        ph_ready = sem("ph_ready")
        pl_ready = sem("pl_ready")
        av_h = sem("av_h")
        av_l = sem("av_l")
        acc_done = sem("acc_done")
        aux_full = [sem("aux_full0"), sem("aux_full1")]
        aux_free = [sem("aux_free0"), sem("aux_free1")]
        mx_chain = sem("mx_chain")
        nm_ready = sem("nm_ready")
        psums_ready = sem("psums_ready")
        o_act, o_dve = sem("o_act"), sem("o_dve")
        norm_done = sem("norm_done")
        x1_ready = sem("x1_ready")
        y_ready = sem("y_ready")

        def chunk(n):
            return ds(n * CH, CH)

        def attend_loop(eng, l, body):
            body(0, "first")
            if l == 1:
                body(1, "mid")
            with eng.Fori(1 + l, NCH - DIST[l]) as n:
                body(n, "mid")
            for n in range(NCH - DIST[l], NCH):
                body(n, "last")

        def body_jobs(l, b, n, kind):
            k, out = [0, 0], []
            for jobs in schedule(l, kind):
                out.append([])
                for name, arg, place in jobs:
                    bank = bank_of(l, name, arg)
                    out[-1].append((aux_base(l, b, n, bank) + k[bank], bank, name, arg, place))
                    k[bank] += 1
            return out

        def late_convolutions(b, n):
            if isinstance(n, int) and n < 2:
                return []
            last = body_jobs(1, b, n - 1, "last" if isinstance(n, int) and n > NCH - DIST[1] else "mid")
            return [j[:4] for jobs in last for j in jobs if j[2] == "Z"]

        def after_last(l, b):
            k, out = [0, 0], []
            for name, arg in tail_jobs(l):
                bank = bank_of(l, name, arg)
                out.append((aux_base(l, b, NCH, bank) + k[bank], bank, name, arg))
                k[bank] += 1
            return out

        def prologue_jobs(l, b):
            order = [(0, "ST", i) for i in range(NST[l])]
            for n in range(1, DIST[l]):
                order += [(n, "ST", 0), (n, "ST", 1), (n - 1, "M", 0)] + [(n, "ST", i) for i in range(2, NST[l])]
            order.append((DIST[l] - 1, "M", 0))
            k, out = [0, 0], []
            for n, name, arg in order:
                bank = arg % 2
                out.append((n, aux_start(l, b, bank) + k[bank], bank, name, arg))
                k[bank] += 1
            return out

        KQ_K, KQ_Q = slice(0, 2 * DK), slice(2 * DK, R3)

        block = ctx.enter_context(nc.Block())

        @block.sync
        def _(sp):
            def load_x(b, c, par, before):
                if before is not None:
                    sp.wait_ge(x_in[par], before)
                sp.dma_start(x_sb[:, :, chunk(c)], x_v[:, ds(b * CT, CT), chunk(c)]).then_inc(x_in[par], 16)

            for c in range(NCH):
                load_x(0, c, c % 2, 16 * (c // 2) if c >= 2 else None)

            def store_y(b, c, par):
                sp.wait_ge(y_ready, CT + (b * NCH + c) * CT + CT)
                sp.dma_start(y_v[:, ds(b * CT, CT), chunk(c)], x_sb[:, :, chunk(c)]).then_inc(y_out[par], 16)

            with sp.Fori(0, B - 1) as b:
                for c in range(NCH):
                    par, k = c % 2, c // 2
                    store_y(b, c, par)
                    stored = sp.snap(sp.to_reg(b * (16 * NCH // 2) + 16 * (k + 1)))
                    before = sp.snap(sp.to_reg(b * (16 * NCH // 2) + 16 * (NCH // 2 + k)))
                    sp.wait_ge(y_out[par], stored)
                    load_x(b + 1, c, par, before)
            for c in range(NCH):
                store_y(B - 1, c, c % 2)
            for par in range(2):
                sp.wait_ge(y_out[par], 16 * B * NCH // 2)

        @block.gpsimd
        def _(pool):
            nc.gpsimd.memset(ident[:, :], 0.0).then_inc(ident_ready, 1)
            nc.gpsimd.memset(ones[:, :], 1.0).then_inc(y_ready, CT)
            nc.gpsimd.memset(nm_wide[:, :, :].bitcast(f32), 0.0)
            pool.wait_ge(ident_ready, 1)
            nc.gpsimd.affine_select(out=ident[:, :], in_=ident[:, :], compare_op=ALU.not_equal, fill=1.0,
                                    base=0, pattern=[[-1, P]], channel_multiplier=1).then_inc(consts_ready, 1)

            def wait_alone(sem_, value):
                value = pool.snap(pool.to_reg(value))
                pool.wait_ge(consts_ready, 1)
                pool.wait_ge(sem_, value)

            def split_x(l, b, c, par):
                wait_alone(xh_ready, chunk_no(l, b, c) + 1)
                nc.gpsimd.tensor_tensor(out=xl[par][:, :, :], in0=x_sb[:, :, chunk(c)],
                                        in1=xh[par][:, :, :].bitcast(f32), op=ALU.subtract).then_inc(xl_ready, 1)

            def split_prob(g, i, wait_buffer):
                pool.wait_ge(ph_ready, g + 1)
                if wait_buffer:
                    pool.wait_ge(av_l, g - 1)
                nc.gpsimd.tensor_tensor(out=prob_l[i][:, :, :], in0=prob[i],
                                        in1=prob_h[i][:, :, :].bitcast(f32), op=ALU.subtract).then_inc(pl_ready, 1)

            def add_x(b, n, a, bank, ct):
                wait_alone(aux_free[bank], ONE + a + 1)
                nc.gpsimd.tensor_tensor(out=x_sb[:, ct, chunk(n - 1)], in0=zc[:, ct, :], in1=x_sb[:, ct, chunk(n - 1)],
                                        op=ALU.add).then_inc(y_ready, 1)

            def attend(l, b, last):
                def body(n, kind):
                    for s in range(STEPS[l]):
                        split_prob(step_no(l, b, n, s), s % 2, kind != "first" or s >= 2)
                        if l == 1 and s == 0:
                            for a, bank, _, ct in late_convolutions(b, n):
                                add_x(b, n - 1, a, bank, ct)
                attend_loop(pool, l, body)
                if l == 0:
                    split_x(1, b, 0, 0)
                else:
                    for a, bank, _, ct in late_convolutions(b, NCH):
                        add_x(b, NCH - 1, a, bank, ct)
                    if not last:
                        split_x(0, b + 1, 0, 0)
                    for a, bank, name, ct in after_last(l, b):
                        if name == "Z":
                            add_x(b, NCH, a, bank, ct)

            def batch(b, last):
                for l in range(2):
                    split_x(l, b, 1, 1)
                    with pool.Fori(1, NCH // 2) as cc:
                        for par in range(2):
                            split_x(l, b, cc * 2 + par, par)
                    attend(l, b, last)

            split_x(0, 0, 0, 0)
            with pool.Fori(0, B - 1) as b:
                batch(b, False)
            batch(B - 1, True)

        @block.scalar
        def _(act):
            act.dma_start(w_sb, w_v).then_inc(w_in, 16)
            act.dma_start(wo[:, :], wo_d).then_inc(cols_in, 16)
            act.dma_start(cols[:, :], cols_d).then_inc(cols_in, 16)
            act.wait_ge(cols_in, 32)
            for ct, first_credit in enumerate((o_act, psums_ready)):
                nc.scalar.activation(gbv[:, ct:ct + 1], cols[:, COL_BV + ct:COL_BV + ct + 1], ACT.Copy,
                                     scale=cols[:, COL_G0:COL_G0 + 1]).then_inc(first_credit, ONE)

            def round_x(l, b, c, par):
                if l == 0:
                    act.wait_ge(x_in[par], b * (16 * NCH // 2) + (c - par) * 8 + 16)
                else:
                    act.wait_ge(x1_ready, ONE + b * NCH + c + 1)
                act.wait_ge(pj_full, CREDIT - FILLS + FILLS * chunk_no(l, b, c))
                nc.scalar.activation(xh[par][:, :, :], x_sb[:, :, chunk(c)], ACT.Copy).then_inc(xh_ready, 1)

            def copy_q_ahead(n):
                nc.scalar.activation(q_ahead[:, :], queries[0:R3, chunk(n)].bitcast(f32),
                                     ACT.Copy).then_inc(q_ahead_ready, 1)

            def high(l, b, c, par):
                pc = chunk_no(l, b, c)

                def full(k):
                    act.wait_ge(pj_full, CREDIT + FILLS * pc + (k + 1))

                def biased(dst, src, rows):
                    nc.scalar.activation(dst, src, ACT.Identity,
                                         bias=cols[rows, COL_KQ[l]:COL_KQ[l] + 1]).then_inc(hi_ready, 1)

                def queries_high():
                    biased(queries[KQ_Q, chunk(c)], pj_kq[par][KQ_Q, :], KQ_Q)
                    biased(queries[0:DK, chunk(c)], pj_kq[par][KQ_Q, :], KQ_Q)

                if l == 0:
                    full(0)
                    biased(keys[KQ_K, chunk(c)], pj_kq[par][KQ_K, :], KQ_K)
                    queries_high()
                    for k in range(2):
                        full(1 + k)
                        nc.scalar.activation(vh[:, ds(c * SUBS + 2 * k, 2), :],
                                             pj_v[k].rearrange("p (t m) -> p t m", t=2), ACT.Copy).then_inc(hi_ready, 1)
                else:
                    act.wait_ge(pj_drained, CREDIT + DRAINS * pc + 2)
                    biased(keys[KQ_K, ds(c * P, P)], ppool[:, :], KQ_K)
                    queries_high()
                    full(2)
                    nc.scalar.activation(vh_flat[:, ds(c * DV, DV)], pj_v[1][:, 0:P], ACT.Copy).then_inc(hi_ready, 1)

            def exps(g, i, wait_buffers):
                act.wait_ge(s_full, g + 1)
                if wait_buffers:
                    act.wait_ge(pl_ready, g - 1)
                    act.wait_ge(acc_done, 2 * g - 2)
                nc.scalar.activation(prob[i], s_ps[i][:, :, :], ACT.Exp).then_inc(p_ready, 1)
                if wait_buffers:
                    act.wait_ge(av_h, g - 1)
                nc.scalar.activation(prob_h[i][:, :, :], s_ps[i][:, :, :], ACT.Exp).then_inc(ph_ready, 1)

            def copy_o(l, b, n):
                act.wait_ge(av_l, step_no(l, b, n, 0))
                if l == 0:
                    act.wait_ge(x1_ready, ONE + b * NCH + n - 1)
                else:
                    act.wait_ge(norm_done, ONE + chunk_no(l, b, n - 1))
                nc.scalar.activation(osb[:, 0, :], o_ps[0][:, :], ACT.Copy).then_inc(o_act, 1)

            def copy_acc(l, b, n):
                act.wait_ge(norm_done, ONE + chunk_no(l, b, n - 1))
                act.wait_ge(acc_done, 2 * step_no(l, b, n, 0))
                nc.scalar.activation(psums[:, :], acc[:, :], ACT.Copy).then_inc(psums_ready, 1)

            def drain(l, b, n, a, bank, name, ct):
                if name == "D2":
                    act.wait_ge(norm_done, ONE + chunk_no(l, b, n - 1))
                    act.wait_ge(aux_full[bank], a + 1)
                    nc.scalar.activation(rb[:, :], aux_bank[bank][:, :], ACT.Copy).then_inc(aux_free[bank], 1)
                elif name == "Z":
                    act.wait_ge(y_ready, CT + (b * NCH + n - 2) * CT + (ct + 1))
                    act.wait_ge(aux_full[bank], a + 1)
                    nc.scalar.activation(zc[:, ct, :], aux_bank[bank][:, :], ACT.Identity, bias=cb[:, ct:ct + 1],
                                         scale=cols[:, COL_G1:COL_G1 + 1]).then_inc(aux_free[bank], 1)

            def round_next(l, b, last):
                if l == 0:
                    round_x(1, b, 0, 0)
                elif not last:
                    round_x(0, b + 1, 0, 0)

            def attend(l, b, last):
                def body(n, kind):
                    jobs = body_jobs(l, b, n, kind)
                    for s in range(STEPS[l]):
                        exps(step_no(l, b, n, s), s % 2, kind != "first" or s >= 2)
                        if s == 0:
                            late = late_convolutions(b, n) if l == 1 else []
                            for j in late[:1]:
                                drain(l, b, n - 1, *j)
                            if kind != "last":
                                for k in range(l + 1):
                                    act.wait_ge(aux_full[k], aux_base(l, b, n, k) - behind_maxima(l, n, k))
                                copy_q_ahead(n + DIST[l])
                            if kind != "first":
                                copy_o(l, b, n)
                                copy_acc(l, b, n)
                            for j in late[1:]:
                                drain(l, b, n - 1, *j)
                        for j in jobs[s - l] if s >= l else ():
                            if j[2] == "D2":
                                drain(l, b, n, *j[:4])
                attend_loop(act, l, body)
                round_next(l, b, last)
                for j in late_convolutions(b, NCH) if l == 1 else ():
                    drain(l, b, NCH - 1, *j)
                copy_acc(l, b, NCH)
                copy_o(l, b, NCH)
                for j in after_last(l, b):
                    drain(l, b, NCH, *j)

            def project(l, b):
                def pair(cc, last):
                    for par in range(2):
                        if not (last and par == 1):
                            round_x(l, b, cc * 2 + (par + 1), 1 - par)
                        high(l, b, cc * 2 + par, par)
                        if l == 0 and isinstance(cc, int) and cc == 0 and par == 0:
                            act.wait_ge(pj_drained, CREDIT + DRAINS * chunk_no(0, b, 0) + 2)
                            copy_q_ahead(0)
                pair(0, False)
                with act.Fori(1, NCH // 2 - 1) as cc:
                    pair(cc, False)
                pair(NCH // 2 - 1, True)

            act.wait_ge(pj_drained, CREDIT)
            round_x(0, 0, 0, 0)

            def batch(b, last):
                project(0, b)
                attend(0, b, last)
                project(1, b)
                for n in range(DIST[1]):
                    if n == 0:
                        act.wait_ge(pj_drained, CREDIT - DRAINS + DRAINS * chunk_no(1, b, NCH))
                    else:
                        for k in range(2):
                            act.wait_ge(aux_full[k], aux_start(1, b, k) + n * STS[1][k])
                    copy_q_ahead(n)
                attend(1, b, last)

            with act.Fori(0, B - 1) as b:
                batch(b, False)
            batch(B - 1, True)

        @block.vector
        def _(dve):
            for k, first_credit in enumerate((aux_free[0], aux_free[1], norm_done, x1_ready)):
                nc.vector.memset(keys[R3:P, ds(k * N // 4, N // 4)].bitcast(f32), 1.0).then_inc(first_credit, ONE)
            dve.wait_ge(w_in, 16)
            nc.vector.tensor_copy(wh[:, :, :], w_sb).then_inc(dve_setup, 1)
            dve.wait_ge(dve_setup, 1)
            nc.vector.tensor_tensor(out=wl[:, :, :], in0=w_sb, in1=wh[:, :, :].bitcast(f32),
                                    op=ALU.subtract).then_inc(w_ready, 1)
            dve.wait_ge(cols_in, 32)
            dve.wait_ge(consts_ready, 1)
            nc.vector.tensor_copy(ident_r[:, :], ident[:, :]).then_inc(o_dve, ONE)
            dve.wait_ge(pj_full, CREDIT)
            nc.vector.tensor_tensor(out=cb[:, :], in0=cols[:, COL_BO:COL_BO + CT], in1=aux[:, 0:CT],
                                    op=ALU.add).then_inc(dve_setup, 1)
            dve.wait_ge(dve_setup, 2)
            nc.vector.tensor_scalar(cb[:, :], cb[:, :], cols[:, COL_G1:COL_G1 + 1], None,
                                    ALU.mult).then_inc(pj_drained, CREDIT)

            def st_drain(a, bank, sub, c):
                dve.wait_ge(aux_full[bank], a + 1)
                nc.vector.tensor_reduce(out=mx[:, sub, c], in_=aux_bank[bank][:, :], axis=AX.X,
                                        op=ALU.max).then_inc(aux_free[bank], 1)

            def finish_max(l, a, bank, target):
                dve.wait_ge(aux_free[bank], ONE + a + 1)
                nc.vector.tensor_reduce(out=nm[:, :], in_=mx[:, :, 0:KEYS[l] // CH], axis=AX.X, op=ALU.max,
                                        negate=True).then_inc(mx_chain, 1)
                dve.wait_ge(mx_chain, 2 * target + 1)
                nc.vector.tensor_copy(nm_wide[:, :, R3], nm[:, :]).then_inc(mx_chain, 1)
                dve.wait_ge(mx_chain, 2 * target + 2)
                nc.vector.tensor_tensor(out=nm_wide[:, :, R3 + 1], in0=nm[:, :], in1=nm_wide[:, :, R3].bitcast(f32),
                                        op=ALU.subtract).then_inc(nm_ready, 1)

            def m_drain(a, n):
                dve.wait_ge(aux_full[0], a + 1)
                nc.vector.tensor_copy(queries[R3:P, chunk(n)], aux[R3:P, :]).then_inc(aux_free[0], 1)

            def low(dst, src, scalar, hi):
                if scalar is None:
                    return nc.vector.tensor_tensor(out=dst, in0=src, in1=hi.bitcast(f32), op=ALU.subtract)
                return nc.vector.scalar_tensor_tensor(out=dst, in0=src, scalar=scalar, in1=hi.bitcast(f32),
                                                      op0=ALU.add, op1=ALU.subtract)

            K1 = slice(0, DK)
            LK = slice(2 * DK, R3)
            LQ = slice(DK, 2 * DK)

            def keys_low(l, src, at):
                low(keys[LK, at], src, cols[K1, COL_KQ[l]:COL_KQ[l] + 1], keys[K1, at]).then_inc(pj_drained, 1)

            def queries_low(l, c, par):
                low(queries[LQ, chunk(c)], pj_kq[par][KQ_Q, :], cols[KQ_Q, COL_KQ[l]:COL_KQ[l] + 1],
                    queries[KQ_Q, chunk(c)]).then_inc(pj_drained, 1)

            def project0(b, c, par, st):

                def high(k):
                    dve.wait_ge(hi_ready, hi_no(0, b, c, k) + 1)

                def maxima(sub):
                    if st:
                        st_drain(aux_maxima(b, c - 1, sub), sub % 2, sub, ds(c - 1, 1))

                maxima(0)
                maxima(1)
                high(0)
                keys_low(0, pj_kq[par][K1, :], chunk(c))
                maxima(2)
                high(2)
                queries_low(0, c, par)
                maxima(3)
                for k in range(2):
                    high(3 + k)
                    tiles = ds(c * SUBS + 2 * k, 2)
                    low(vl[:, tiles, :], pj_v[k].rearrange("p (t m) -> p t m", t=2), None,
                        vh[:, tiles, :]).then_inc(pj_drained, 1)

            def pool_max(dst, src):
                return nc.vector.tensor_reduce(
                    out=dst.rearrange("p (h w) -> p h w", w=PW),
                    in_=src.rearrange("p (h a w b) -> p h w a b", a=2, b=2, w=PW), axis=AX.XY, op=ALU.max)

            def project1(b, c, par):
                pc = chunk_no(1, b, c)
                dve.wait_ge(pj_drained, CREDIT + DRAINS * pc)
                dve.wait_ge(pj_full, CREDIT + FILLS * pc + 1)
                pool_max(gpool[:, :], pj_v[0]).then_inc(pj_drained, 1)
                dve.wait_ge(pj_full, CREDIT + FILLS * pc + 2)
                pool_max(ppool[:, :], pj_kq[par][KQ_K, :]).then_inc(pj_drained, 1)
                dve.wait_ge(hi_ready, hi_no(1, b, c, 0) + 1)
                low(keys[LK, ds(c * P, P)], ppool[K1, :], cols[K1, COL_KQ[1]:COL_KQ[1] + 1], keys[K1, ds(c * P, P)])
                dve.wait_ge(hi_ready, hi_no(1, b, c, 2) + 1)
                queries_low(1, c, par)
                dve.wait_ge(hi_ready, hi_no(1, b, c, 3) + 1)
                low(vl_flat[:, ds(c * DV, DV)], pj_v[1][:, 0:P], None,
                    vh_flat[:, ds(c * DV, DV)]).then_inc(pj_drained, 1)

            def add_prob(l, b, n, s, t):
                g, i = step_no(l, b, n, s), s % 2
                if t == 0:
                    dve.wait_ge(p_ready, g + 1)
                if s == 0 and t == 0:
                    dve.wait_ge(psums_ready, ONE + chunk_no(l, b, n))
                    nc.vector.tensor_copy(acc[:, :], prob[i][:, 0, :]).then_inc(acc_done, 1)
                else:
                    dve.wait_ge(acc_done, 2 * g + t)
                    nc.vector.tensor_tensor(out=acc[:, :], in0=prob[i][:, t, :], in1=acc[:, :],
                                            op=ALU.add).then_inc(acc_done, 1)

            def drain(l, b, n, a, bank, name, arg):
                if name == "ST":
                    st_drain(a, bank, arg % SUBS, slice(arg // SUBS, arg // SUBS + 1))
                elif name == "M":
                    m_drain(a, n + DIST[l])
                elif name == "D1":
                    dve.wait_ge(aux_full[bank], a + 1)
                    nc.vector.reciprocal(rsum[:, :], aux_bank[bank][:, 0:SUBS]).then_inc(aux_free[bank], 1)

            def normalise(l, b, n, k):
                if l == 1:
                    nc.vector.tensor_tensor(out=osb[:, 1, :], in0=osb[:, 0, :], in1=rb[:, :],
                                            op=ALU.mult).then_inc(norm_done, 1)
                elif k < CT:
                    ins = nc.vector.scalar_tensor_tensor(out=osb[:, k, :], in0=osb[:, k, :],
                                                         scalar=cols[:, COL_G0:COL_G0 + 1], in1=rb[:, :],
                                                         op0=ALU.mult, op1=ALU.mult)
                    if k == CT - 1:
                        ins.then_inc(norm_done, 1)
                else:
                    ct = k - CT
                    dve.wait_ge(norm_done, ONE + chunk_no(0, b, n))
                    ins = nc.vector.scalar_tensor_tensor(
                        out=x_sb[:, ct, chunk(n - 1)], in0=osb[:, ct, :], scalar=gbv[:, ct:ct + 1],
                        in1=x_sb[:, ct, chunk(n - 1)], op0=ALU.add, op1=ALU.add)
                    if ct == CT - 1:
                        ins.then_inc(x1_ready, 1)

            def before_normalise(l, b, n, a, bank):
                dve.wait_ge(aux_free[bank], ONE + a + 1)
                dve.wait_ge(o_act, ONE + chunk_no(l, b, n))

            def copy_o(b, n):
                dve.wait_ge(av_l, step_no(0, b, n, 0))
                dve.wait_ge(x1_ready, ONE + b * NCH + n - 1)
                nc.vector.tensor_copy(osb[:, 1, :], o_ps[1][:, :]).then_inc(o_dve, 1)

            def attend(l, b):
                def body(n, kind):
                    jobs = body_jobs(l, b, n, kind)
                    sums = [j[:2] for step in jobs for j in step if j[2] == "D2"]
                    if l == 0 and kind != "first":
                        copy_o(b, n)
                    for s in range(STEPS[l]):
                        if l == 1 and s == STEPS[1] - 1:
                            for k in range(2):
                                add_prob(l, b, n, s, k)
                            for j in jobs[s]:
                                if j[2] == "M":
                                    drain(l, b, n, *j[:4])
                            continue
                        mine = [j[:4] for j in jobs[s] if j[2] in ("ST", "M", "D1")]
                        for k in range(max(len(mine), 3)):
                            if l == 1 and kind != "first" and s in NORM_STEPS[l] and k == NORM_AT:
                                before_normalise(l, b, n, *sums[0])
                                normalise(l, b, n, 0)
                            if k < len(mine):
                                drain(l, b, n, *mine[k])
                                if mine[k][2:] == ("ST", NST[l] - 1):
                                    finish_max(l, *mine[k][:2], chunk_no(l, b, n + DIST[l]))
                            if k < 2:
                                add_prob(l, b, n, s, k)
                        if l == 0 and kind != "first" and s in NORM_STEPS[l]:
                            k = NORM_STEPS[l].index(s)
                            if k == 0:
                                before_normalise(l, b, n, *sums[0])
                            normalise(l, b, n, k)
                attend_loop(dve, l, body)
                if l == 0:
                    copy_o(b, NCH)
                jobs = after_last(l, b)
                drain(l, b, NCH, *jobs[0])
                before_normalise(l, b, NCH, *jobs[1][:2])
                for k in range(len(NORM_STEPS[l])):
                    normalise(l, b, NCH, k)

            def prologue(l, b, jobs):
                for n, a, bank, name, arg in jobs:
                    if name == "M":
                        m_drain(a, n)
                    else:
                        st_drain(a, bank, arg % SUBS, slice(arg // SUBS, arg // SUBS + 1))
                        if arg == NST[l] - 1:
                            finish_max(l, a, bank, chunk_no(l, b, n))

            with dve.Fori(0, B) as b:
                project0(b, 0, 0, False)
                project0(b, 1, 1, True)
                with dve.Fori(1, NCH // 2) as cc:
                    for par in range(2):
                        project0(b, cc * 2 + par, par, True)
                prologue(0, b, prologue_jobs(0, b)[-1 - SUBS:])
                attend(0, b)
                with dve.Fori(0, NCH // 2) as cc:
                    for par in range(2):
                        project1(b, cc * 2 + par, par)
                prologue(1, b, prologue_jobs(1, b))
                attend(1, b)

        @block.tensor
        def _(pe):
            mm = nc.tensor.matmul
            pe.wait_ge(cols_in, 32)
            for ct in range(CT):
                last = mm(aux[:, ct:ct + 1], wo[:, ct * P:(ct + 1) * P], cols[:, COL_BG:COL_BG + 1],
                          start=True, stop=True)
            last.then_inc(pj_full, CREDIT)
            pe.wait_ge(w_ready, 1)
            pe.wait_ge(pj_drained, CREDIT)

            def st_job(a, bank, sub, c):
                pe.wait_ge(aux_free[bank], ONE + a)
                mm(aux_bank[bank][:, :], q_ahead[:, sub * P:(sub + 1) * P], keys[0:R3, chunk(c)],
                   start=True, stop=True).then_inc(aux_full[bank], 1)

            def m_job(a, target):
                pe.wait_ge(aux_free[0], ONE + a)
                pe.wait_ge(nm_ready, target + 1)
                for s in range(SUBS):
                    last = mm(aux[:, s * P:(s + 1) * P], nm_wide[:, s, :], ident_r[:, :], start=True, stop=True)
                last.then_inc(aux_full[0], 1)

            def conv(dst, w0, width, par, wait):
                first = True
                for kt in range(CT):
                    for w in (wh, wl):
                        mm(dst, w[:, kt, w0:w0 + width], xh[par][:, kt, :], start=first, stop=False)
                        first = False
                if wait is not None:
                    pe.wait_ge(xl_ready, wait)
                for kt in range(CT):
                    last = mm(dst, wh[:, kt, w0:w0 + width], xl[par][:, kt, :], start=False, stop=kt == CT - 1)
                return last

            def project0(b, c, par, st):
                pc = chunk_no(0, b, c)

                def drained(k):
                    pe.wait_ge(pj_drained, CREDIT - DRAINS + DRAINS * pc + (k + 1))

                def maxima(sub):
                    if st:
                        st_job(aux_maxima(b, c - 1, sub), sub % 2, sub, c - 1)

                if st:
                    drained(0)
                    pe.wait_ge(q_ahead_ready, chunk_no(0, b, 0) + 1)
                maxima(0)
                pe.wait_ge(xh_ready, pc + 1)
                conv(pj_kq[par][0:R3, :], W_KQ[0], R3, par, pc + 1).then_inc(pj_full, 1)
                maxima(1)
                for t in range(SUBS):
                    if t % 2 == 0:
                        drained(2 + t // 2)
                    pos = slice(t * P, (t + 1) * P)
                    dst = pj_v[t // 2][:, t % 2 * C:(t % 2 + 1) * C]
                    first = True
                    for kt in range(CT):
                        for w in (wh, wl):
                            mm(dst, xh[par][:, kt, pos], w[:, kt, W_V:W_V + C], start=first, stop=False)
                            first = False
                    for kt in range(CT):
                        last = mm(dst, xl[par][:, kt, pos], wh[:, kt, W_V:W_V + C], start=False, stop=kt == CT - 1)
                    if t % 2 == 1:
                        last.then_inc(pj_full, 1)
                    if t in (1, 2):
                        maxima(t + 1)

            def project1(b, c, par):
                pc = chunk_no(1, b, c)
                pe.wait_ge(pj_drained, CREDIT - DRAINS + DRAINS * pc + 1)
                pe.wait_ge(xh_ready, pc + 1)
                conv(pj_v[0], W_G, DV, par, pc + 1).then_inc(pj_full, 1)
                conv(pj_kq[par][0:R3, :], W_KQ[1], R3, par, None).then_inc(pj_full, 1)
                pe.wait_ge(pj_drained, CREDIT + DRAINS * pc + 1)
                nc.tensor.transpose(pj_v[1][:, 0:P], gpool[:, :], ident[:, :]).then_inc(pj_full, 1)

            def scores(l, n, s):
                i = s % 2
                for t in range(2):
                    kt = 2 * s + t
                    last = mm(s_ps[i][:, t, :], keys[:, kt * P:(kt + 1) * P], queries[:, chunk(n)],
                              start=True, stop=True)
                last.then_inc(s_full, 1)

            def av(l, s, low, k):
                if low:
                    t, ct = k // VT[l], k % VT[l]
                else:
                    t, ct = k // (2 * VT[l]), k // 2 % VT[l]
                kt = 2 * s + t
                at = (kt * VT[l] + ct) * P
                value = (vl_flat if not low and k % 2 else vh_flat)[:, at:at + P]
                ins = mm(o_ps[ct][:, :], value, (prob_l if low else prob_h)[s % 2][:, t, :],
                         start=not low and k % 2 == 0 and kt == 0, stop=low and kt == KT[l] - 1)
                if k == (2 if low else 4) * VT[l] - 1:
                    ins.then_inc(av_l if low else av_h, 1)

            def job(l, b, n, a, bank, name, arg, rsum_job):
                dst = aux_bank[bank]
                if name == "ST":
                    if arg == 0:
                        pe.wait_ge(q_ahead_ready, chunk_no(l, b, n + DIST[l]) + 1)
                    st_job(a, bank, arg % SUBS, arg // SUBS)
                    return
                if name == "M":
                    m_job(a, chunk_no(l, b, n + DIST[l]))
                    return
                pe.wait_ge(aux_free[bank], ONE + a)
                if name == "D1":
                    pe.wait_ge(psums_ready, ONE + chunk_no(l, b, n))
                    for s in range(SUBS):
                        last = mm(dst[:, s:s + 1], psums[:, s * P:(s + 1) * P], ones[:, 0:1], start=True, stop=True)
                elif name == "D2":
                    pe.wait_ge(aux_free[rsum_job[1]], ONE + rsum_job[0] + 1)
                    for s in range(SUBS):
                        last = mm(dst[:, s * P:(s + 1) * P], rsum[:, s:s + 1].broadcast_to([P, P]), ident[:, :],
                                  start=True, stop=True)
                else:
                    pe.wait_ge(norm_done, ONE + chunk_no(l, b, n))
                    last = mm(dst[:, :], wo[:, arg * P:(arg + 1) * P], osb[:, 1, :], start=True, stop=True)
                last.then_inc(aux_full[bank], 1)

            def attend(l, b):
                def body(n, kind):
                    jobs = body_jobs(l, b, n, kind)
                    rsum_job = [j for step in jobs for j in step if j[2] == "D1"][:1] or [None]
                    rsum_job = rsum_job[0]
                    for s in range(STEPS[l]):
                        g = step_no(l, b, n, s)

                        def jobs_at(place):
                            for j in jobs[s]:
                                if j[4] == place:
                                    job(l, b, n, *j[:4], rsum_job)

                        if s + 1 < STEPS[l]:
                            scores(l, n, s + 1)
                        elif not (isinstance(n, int) and n == NCH - 1):
                            pe.wait_ge(aux_free[0], ONE + (aux_base(l, b, n + 1) if l == 0 else aux_base(l, b, n)))
                            scores(l, n + 1, 0)
                        place = 0
                        for k in range(2 * VT[l]):
                            jobs_at(place)
                            place += 1
                            if s:
                                if k == 0:
                                    pe.wait_ge(pl_ready, g)
                                av(l, s - 1, True, k)
                        for k in range(4 * VT[l]):
                            jobs_at(place)
                            place += 1
                            if k == 0:
                                if s == 0:
                                    pe.wait_ge(o_act, ONE + chunk_no(l, b, n))
                                    if l == 0:
                                        pe.wait_ge(o_dve, ONE + b * NCH + n)
                                pe.wait_ge(ph_ready, g + 1)
                            av(l, s, False, k)
                        jobs_at(place)
                    pe.wait_ge(pl_ready, step_no(l, b, n, STEPS[l]))
                    for k in range(2 * VT[l]):
                        av(l, STEPS[l] - 1, True, k)

                if l == 0:
                    pe.wait_ge(pj_drained, CREDIT + DRAINS * chunk_no(l, b, NCH))
                    pe.wait_ge(aux_free[0], ONE + aux_base(l, b, 0))
                    pe.wait_ge(aux_free[1], ONE + aux_base(0, b, 0, 1))
                    scores(l, 0, 0)
                attend_loop(pe, l, body)
                jobs = after_last(l, b)
                for j in jobs:
                    job(l, b, NCH, *j, jobs[0])

            with pe.Fori(0, B) as b:
                project0(b, 0, 0, False)
                project0(b, 1, 1, True)
                with pe.Fori(1, NCH // 2) as cc:
                    for par in range(2):
                        project0(b, cc * 2 + par, par, True)
                pe.wait_ge(pj_drained, CREDIT - DRAINS + DRAINS * chunk_no(0, b, NCH) + 1)
                for n, a, bank, name, arg in prologue_jobs(0, b)[-1 - SUBS:]:
                    if name == "ST":
                        st_job(a, bank, arg % SUBS, arg // SUBS)
                    else:
                        m_job(a, chunk_no(0, b, n))
                attend(0, b)
                with pe.Fori(0, NCH // 2) as cc:
                    for par in range(2):
                        project1(b, cc * 2 + par, par)
                pe.wait_ge(o_dve, ONE + b * NCH + NCH)
                for n, a, bank, name, arg in prologue_jobs(1, b):
                    if name == "M":
                        m_job(a, chunk_no(1, b, n))
                        m_before = a
                        continue
                    if arg == 0:
                        pe.wait_ge(q_ahead_ready, chunk_no(1, b, n) + 1)
                    elif n == 0 and arg == SUBS:
                        pe.wait_ge(pj_drained, CREDIT + DRAINS * chunk_no(1, b, NCH))
                    st_job(a, bank, arg % SUBS, arg // SUBS)
                    if n == 1 and arg == 3:
                        pe.wait_ge(aux_free[0], ONE + m_before + 1)
                        scores(1, 0, 0)
                attend(1, b)


def kernel(x, L0_conv_Wq, L0_conv_bq, L0_conv_Wk, L0_conv_bk, L0_conv_Wv, L0_conv_bv, L0_conv_gamma,
           L1_conv_theta_w, L1_conv_theta_b, L1_conv_phi_w, L1_conv_phi_b, L1_conv_g_w, L1_conv_g_b,
           L1_conv_out_w, L1_conv_out_b, L1_conv_gamma):
    import numpy as np
    import concourse.bacc as bacc
    from concourse.bass_utils import run_bass_kernel_spmd

    def stacked(k, q, axis):
        return np.concatenate([np.asarray(k), np.asarray(k), np.asarray(q)], axis=axis)

    w = np.concatenate([stacked(L0_conv_Wq, L0_conv_Wk, 0).T, stacked(L1_conv_phi_w, L1_conv_theta_w, 0).T,
                        np.asarray(L0_conv_Wv).T, np.asarray(L1_conv_g_w).T], axis=1)
    cols = np.zeros((P, NCOLS), np.float32)
    cols[:R3, COL_KQ[0]] = stacked(L0_conv_bq, L0_conv_bk, 0)
    cols[:R3, COL_KQ[1]] = stacked(L1_conv_phi_b, L1_conv_theta_b, 0)
    cols[:, COL_BV:COL_BV + CT] = np.asarray(L0_conv_bv).reshape(CT, P).T
    cols[:, COL_BG] = np.asarray(L1_conv_g_b)
    cols[:, COL_BO:COL_BO + CT] = np.asarray(L1_conv_out_b).reshape(CT, P).T
    cols[:, COL_G0] = np.broadcast_to(np.asarray(L0_conv_gamma), (P,))
    cols[:, COL_G1] = np.broadcast_to(np.asarray(L1_conv_gamma), (P,))
    arrays = {
        "x": np.ascontiguousarray(np.asarray(x).reshape(B, C, N)),
        "w_in": np.ascontiguousarray(w),
        "w_out": np.ascontiguousarray(np.asarray(L1_conv_out_w).T),
        "columns": cols,
    }
    f32 = mybir.dt.float32
    nc = bacc.Bacc("TRN2", target_bir_lowering=False, num_devices=1)
    ins = [nc.dram_tensor(k, a.shape, f32, kind="ExternalInput").ap() for k, a in arrays.items()]
    y = nc.dram_tensor("y", (B, C, N), f32, kind="ExternalOutput").ap()
    build(nc, *ins, y)
    r = run_bass_kernel_spmd(nc, [arrays], core_ids=[0])
    return r.results[0]["y"].reshape(B, C, IMG_W, IMG_W)
```
